# Optimizing a Trainium2 kernel written in Bass

```python
import numpy as np
import jax
import jax.numpy as jnp

def _softmax(x, axis=-1):
    return jax.nn.softmax(x, axis=axis)

def _gelu(x):
    return jax.nn.gelu(x, approximate=True)

def _silu(x):
    return jax.nn.silu(x)

def _sigmoid(x):
    return jax.nn.sigmoid(x)

def _layernorm(x, axis=-1, eps=1e-05):
    m = jnp.mean(x, axis=axis, keepdims=True)
    v = jnp.var(x, axis=axis, keepdims=True)
    return (x - m) / jnp.sqrt(v + eps)

def _scatter_add(tgt, idx, src, axis=0):
    return tgt.at[idx].add(src)

def _segment_sum(src, seg, n):
    return jax.ops.segment_sum(src, seg, n)
kernel_name = 'mk_adj_preln_d4_adj_r2_66bd62'

def setup_inputs(seed: int=0):
    np.random.seed(seed)
    _w = jnp.asarray

    def _rec_inputs():
        import jax
        import jax.numpy as jnp
        _gk = jax.random.key(seed)
        x = -0.0002928 + 1 * jax.random.normal(jax.random.fold_in(_gk, 1), (8, 1024, 64), jnp.float32)
        _a = jax.random.bernoulli(jax.random.fold_in(_gk, 2), 0.00390625, (1024, 1024))
        _a = jnp.logical_or(_a, jnp.swapaxes(_a, -1, -2))
        _a = jnp.logical_or(_a, jnp.eye(1024, dtype=bool))
        _af = _a.astype(jnp.float32)
        _af = _af / jnp.maximum(_af.sum(-1, keepdims=True), 1.0)
        adj = _af
        return (x, adj)
    x, adj = _rec_inputs()

    def _L0_gnn_setup():
        import jax, jax.numpy as jnp
        import numpy as np
        key = jax.random.key(seed)
        ks = jax.random.split(key, 5)
        B, N, IN, OUT, K, D = (32, 1024, 64, 64, 3, 16)
        x = jax.random.normal(ks[0], (B, N, IN), dtype=jnp.float32)
        A = jax.random.uniform(ks[1], (N, N), dtype=jnp.float32)
        A = A / jnp.sum(A, axis=-1, keepdims=True)
        embedding = jax.random.normal(ks[2], (N, D), dtype=jnp.float32) * 0.3
        weight = jax.random.normal(ks[3], (D, K, IN, OUT), dtype=jnp.float32) * 0.1
        bias = jax.random.normal(ks[4], (D, OUT), dtype=jnp.float32) * 0.1
        return {'x': x, 'A': A, 'embedding': embedding, 'weight': weight, 'bias': bias}
    _L0_gnn_all = _L0_gnn_setup()
    _L0_gnn_in = {k: v for k, v in _L0_gnn_all.items() if k in ('embedding', 'weight', 'bias')}
    del _L0_gnn_all

    def _L1_gnn_setup():
        import jax, jax.numpy as jnp
        import numpy as np
        key = jax.random.key(seed)
        k1, k2, k3 = jax.random.split(key, 3)
        B, N, D = (4, 4096, 64)
        X = jax.random.normal(k1, (B, N, D), dtype=jnp.float32)
        A = jax.random.uniform(k2, (N, N), dtype=jnp.float32)
        W = jax.random.truncated_normal(k3, -2.0, 2.0, (D, D), dtype=jnp.float32) * 0.05
        return {'X': X, 'A': A, 'W': W}
    _L1_gnn_all = _L1_gnn_setup()
    _L1_gnn_in = {k: v for k, v in _L1_gnn_all.items() if k in ('W',)}
    del _L1_gnn_all

    def _L2_gnn_setup():
        import jax, jax.numpy as jnp
        import numpy as np
        NEG_INF = -1e+16

        def gat_layer(x, graph, W, b):
            h = x @ W
            s = jnp.einsum('bnd,bmd->bnm', h, h) * graph
            s = jnp.where(s == 0.0, NEG_INF, s)
            a = jax.nn.softmax(s, axis=2)
            return jnp.einsum('bnm,bmd->bnd', a, h) + b
        key = jax.random.key(seed)
        k1, k2, k3, k4, k5, k6 = jax.random.split(key, 6)
        B, N, C_IN, HID, HEADS, C_OUT = (16, 512, 64, 128, 8, 64)
        flow_x = jax.random.normal(k1, (B, N, C_IN), dtype=jnp.float32)
        graph = jax.random.randint(k2, (N, N), 0, 2).astype(jnp.float32)
        Wh = jax.random.normal(k3, (HEADS, C_IN, HID), dtype=jnp.float32)
        bh = jax.random.normal(k4, (HEADS, HID), dtype=jnp.float32)
        W_out = jax.random.normal(k5, (HID * HEADS, C_OUT), dtype=jnp.float32)
        b_out = jax.random.normal(k6, (C_OUT,), dtype=jnp.float32)
        return {'flow_x': flow_x, 'graph': graph, 'Wh': Wh, 'bh': bh, 'W_out': W_out, 'b_out': b_out}
    _L2_gnn_all = _L2_gnn_setup()
    _L2_gnn_in = {k: v for k, v in _L2_gnn_all.items() if k in ('Wh', 'bh', 'W_out', 'b_out')}
    del _L2_gnn_all

    def _L3_gnn_setup():
        import jax, jax.numpy as jnp
        import numpy as np
        B, N, F, L = (4, 4096, 64, 2)
        key = jax.random.key(seed)
        k1, k2, k3 = jax.random.split(key, 3)
        x = jax.random.normal(k1, (B, N, F), dtype=jnp.float32)
        net_params = jax.random.normal(k2, (L * F * F,), dtype=jnp.float32)
        A = jax.random.normal(k3, (N, N), dtype=jnp.float32)
        return {'x': x, 't': 0, 'net_params': net_params, 'A': A}
    _L3_gnn_all = _L3_gnn_setup()
    _L3_gnn_in = {k: v for k, v in _L3_gnn_all.items() if k in ('net_params',)}
    del _L3_gnn_all
    return {'x': x, 'adj': adj, 'L0_gnn_embedding': _L0_gnn_in['embedding'], 'L0_gnn_weight': _L0_gnn_in['weight'], 'L0_gnn_bias': _L0_gnn_in['bias'], 'L1_gnn_W': _L1_gnn_in['W'], 'L2_gnn_Wh': _L2_gnn_in['Wh'], 'L2_gnn_bh': _L2_gnn_in['bh'], 'L2_gnn_W_out': _L2_gnn_in['W_out'], 'L2_gnn_b_out': _L2_gnn_in['b_out'], 'L3_gnn_net_params': _L3_gnn_in['net_params']}

def reference(x, adj, L0_gnn_embedding, L0_gnn_weight, L0_gnn_bias, L1_gnn_W, L2_gnn_Wh, L2_gnn_bh, L2_gnn_W_out, L2_gnn_b_out, L3_gnn_net_params):
    import jax
    import jax.numpy as jnp

    def _L0_gnn_ref(x, A, embedding, weight, bias):
        import jax, jax.numpy as jnp
        import numpy as np
        K = weight.shape[1]
        N = A.shape[-2]
        w = jnp.einsum('nd,dkio->nkio', embedding, weight)
        b = jnp.einsum('nd,do->no', embedding, bias)
        As = [jnp.eye(N, dtype=x.dtype)]
        if K > 1:
            As.append(A)
        for _ in range(2, K):
            As.append(2.0 * (A @ As[-1]) - As[-2])
        A_stack = jnp.stack(As, 0)
        x_g = jnp.einsum('knm,bmc->bnkc', A_stack, x)
        out = jnp.einsum('bnki,nkio->bno', x_g, w)
        return out + b

    def _L1_gnn_ref(X, A, W):
        import jax, jax.numpy as jnp
        import numpy as np
        n = A.shape[0]
        A_td = A + jnp.eye(n, dtype=A.dtype)
        deg = jnp.sum(A_td, axis=1)
        dinv = jax.lax.rsqrt(deg)
        A_hat = dinv[:, None] * A_td * dinv[None, :]
        H = jnp.einsum('bmd,nm->bnd', X, A_hat)
        X_p = jnp.einsum('bnd,kd->bnk', H, W)
        return X_p

    def _L2_gnn_ref(flow_x, graph, Wh, bh, W_out, b_out):
        import jax, jax.numpy as jnp
        import numpy as np
        NEG_INF = -1e+16

        def gat_layer(x, graph, W, b):
            h = x @ W
            s = jnp.einsum('bnd,bmd->bnm', h, h) * graph
            s = jnp.where(s == 0.0, NEG_INF, s)
            a = jax.nn.softmax(s, axis=2)
            return jnp.einsum('bnm,bmd->bnd', a, h) + b
        heads = jax.vmap(lambda W, b: gat_layer(flow_x, graph, W, b))(Wh, bh)
        H, B, N, D = heads.shape
        cat = jnp.moveaxis(heads, 0, 2).reshape(B, N, H * D)
        x = jax.nn.leaky_relu(cat, negative_slope=0.01)
        out = gat_layer(x, graph, W_out, b_out)
        return jax.nn.leaky_relu(out, negative_slope=0.01)

    def _L3_gnn_ref(x, t, net_params, A):
        import jax, jax.numpy as jnp
        import numpy as np
        B, N, F, L = (4, 4096, 64, 2)
        weights = net_params.reshape(L, F, F)
        z = x.reshape(-1, A.shape[1], F)
        for i in range(L):
            h = jnp.einsum('mn,bnf->bmf', A, z)
            z = jnp.einsum('bmf,fg->bmg', h, weights[i])
            z = jax.nn.relu(z)
        return z
    h = jnp.maximum(_layernorm(x, axis=-1), 0.0)
    x = x + _L0_gnn_ref(h, adj, L0_gnn_embedding, L0_gnn_weight, L0_gnn_bias)
    h = jnp.maximum(_layernorm(x, axis=-1), 0.0)
    x = x + _L1_gnn_ref(h, adj, L1_gnn_W)
    h = jnp.maximum(_layernorm(x, axis=-1), 0.0)
    x = x + _L2_gnn_ref(h, adj, L2_gnn_Wh, L2_gnn_bh, L2_gnn_W_out, L2_gnn_b_out)
    h = jnp.maximum(_layernorm(x, axis=-1), 0.0)
    x = x + _L3_gnn_ref(h, 0, L3_gnn_net_params, adj)
    return x

_drawn_inputs = setup_inputs


def setup_inputs(seed=0):
    import zlib

    import numpy as np

    out = dict(_drawn_inputs(seed))
    spreads = {}
    factors = {'L2_gnn_b_out': 6.482}
    for name, (base, spread) in spreads.items():
        noise = np.random.default_rng([zlib.crc32(name.encode()), seed]).standard_normal(out[name].shape)
        drawn = base * np.exp(spread * noise) if base else spread * noise
        out[name] = jnp.asarray(drawn.astype(out[name].dtype))
    for name, factor in factors.items():
        out[name] = (out[name] * factor).astype(out[name].dtype)
    return out
```

```python
from contextlib import ExitStack, contextmanager

import concourse.bass as bass
from concourse import mybir

F32 = mybir.dt.float32
F32R = mybir.dt.float32r
ALU = mybir.AluOpType
ACT = mybir.ActivationFunctionType
AX = mybir.AxisListType

P = 128
NEG_INF = -1e16
EPS = 1e-5
SLOPE = 0.01


def wait_apart(eng, sem, value, met):
    eng.wait_ge(*met)
    eng.wait_ge(sem, value)


class Count:

    def __init__(self, sem):
        self.sem, self.value = sem, 0

    def add(self, instruction):
        instruction.then_inc(self.sem, 1)
        self.value = self.value + 1

    @contextmanager
    def over(self, eng, trips, each):
        start = self.value
        with eng.Fori(0, trips) as i:
            self.value = start + i * each
            yield i
        self.value = start + trips * each


def build_kernel(nc, x, adj, emb, l0_w, l0_b, l1_w, wh, bh, w_out, b_out, l3_w, out):
    B, N, C = x.shape
    D, K, _, O = l0_w.shape
    H, _, HID = wh.shape
    T = N // P
    BC = B * C
    HN = N // 2
    G2 = 2 * C
    assert BC == HN == 512 and G2 == P and HID == P and K == 3

    with ExitStack() as whole:
        def sb(name, shape, dt=F32, ctx=whole):
            return ctx.enter_context(nc.sbuf_tensor(name, shape, dt))

        def ps(name, shape, ctx=whole):
            return ctx.enter_context(nc.psum_tensor(name, shape, F32))

        adjs = sb("adjs", [P, T, N])
        res = sb("res", [P, T, B, C])
        act = sb("act", [P, T, B, C])
        emb_s = sb("emb_s", [P, T, D])
        ident = sb("ident", [P, P])
        fold = sb("fold", [P, P])
        ones = sb("ones", [P, P])
        dinv = sb("dinv", [P, T])
        bd1 = sb("bd1", [P, P])
        bd3 = sb("bd3", [P, 2, P])
        w_cat = sb("w_cat", [P, H, HID + 1])
        m_split = sb("m_split", [P, H, P], F32R)
        w_proj = sb("w_proj", [P, H, O])
        b_proj = sb("b_proj", [P, O])
        tiny = sb("tiny", [P, 2])

        def sems(ctx, *names):
            return [ctx.enter_context(nc.semaphore(n)) for n in names]

        def split_halves(ap):
            return ap.rearrange("p (t x) -> p t x", t=2)

        with ExitStack() as ctx:
            w1_rows = sb("w1_rows", [C, 2, C], ctx=ctx)
            wh_rows = sb("wh_rows", [C, H, HID], ctx=ctx)
            bh_rows = sb("bh_rows", [H, HID], ctx=ctx)
            wh_t = sb("wh_t", [P, 2, 2, C], ctx=ctx)
            m_high = sb("m_high", [P, P], F32R, ctx=ctx)
            deg = sb("deg", [P, T], ctx=ctx)
            std = sb("std", [P, T], ctx=ctx)
            pa = ps("pa", [P, 512], ctx)
            pb = ps("pb", [P, 512], ctx)
            loaded, adj_in, zeroed, ident_ok, consts, pe_done, act_done, dve_done = sems(
                ctx, "loaded", "adj_in", "zeroed", "ident_ok", "consts", "prep_pe", "prep_act", "prep_dve")
            block = ctx.enter_context(nc.Block())
            SMALL = 13 + T

            @block.sync
            def _(sp):
                for t in range(T):
                    sp.dma_start(res[:, t], x.rearrange("b (t p) c -> t p b c", p=P)[t]).then_inc(loaded, 16)
                for t in range(T):
                    sp.dma_start(adjs[:, t, :], adj[t * P:(t + 1) * P, :]).then_inc(adj_in, 16)
                sp.wait_ge(adj_in, 16 * T)
                sp.wait_ge(loaded, 16 * SMALL)

            @block.gpsimd
            def _(pool):
                for tile in (ident, fold, bd1, bd3):
                    nc.gpsimd.memset(tile[:], 0.0).then_inc(zeroed, 1)
                nc.gpsimd.memset(ones[:], 1.0).then_inc(consts, 1)
                nc.gpsimd.memset(tiny[:], EPS).then_inc(consts, 1)
                pool.wait_ge(zeroed, 4)
                nc.gpsimd.affine_select(out=ident[:], in_=ident[:], compare_op=ALU.not_equal, fill=1.0, base=0,
                                        pattern=[[-1, P]], channel_multiplier=1).then_inc(ident_ok, 1)
                for n, base in enumerate((0, C, -C)):
                    if n:
                        pool.wait_ge(consts, 2 + n)
                    nc.gpsimd.affine_select(out=fold[:], in_=fold[:], compare_op=ALU.not_equal, fill=1.0,
                                            base=base, pattern=[[-1, P]], channel_multiplier=1).then_inc(consts, 1)

            @block.scalar
            def _(a):
                a.dma_start(emb_s[:], emb.rearrange("(t p) d -> p t d", p=P)).then_inc(loaded, 16)
                for k in range(2):
                    a.dma_start(w1_rows[:, k, :], l1_w).then_inc(loaded, 16)
                a.dma_start(wh_rows[:], wh.rearrange("h c d -> c h d")).then_inc(loaded, 16)
                a.dma_start(bh_rows[:], bh).then_inc(loaded, 16)
                for k in range(2):
                    a.dma_start(w_cat[k * C:(k + 1) * C, :, 0:HID], wh.rearrange("h c d -> c h d")).then_inc(loaded, 16)
                a.dma_start(w_proj[:], w_out.rearrange("(h d) o -> d h o", d=P)).then_inc(loaded, 16)
                a.dma_start(b_proj[:], b_out.partition_broadcast(P)).then_inc(loaded, 16)
                a.wait_ge(zeroed, 4)
                for layer in range(2):
                    for k in range(2):
                        a.dma_start(bd3[k * C:(k + 1) * C, layer, k * C:(k + 1) * C],
                                    l3_w.rearrange("(l f g) -> l f g", l=2, f=C)[layer]).then_inc(loaded, 16)
                a.wait_ge(pe_done, 1)
                for k in range(2):
                    nc.scalar.activation(bd1[k * C:(k + 1) * C, k * C:(k + 1) * C],
                                         pa[k * C:(k + 1) * C, 0:C], ACT.Copy).then_inc(act_done, 1)
                a.wait_ge(pe_done, 2)
                nc.scalar.activation(w_cat[:, :, HID], pb[:, 0:H], ACT.Copy).then_inc(act_done, 1)
                for h in range(H):
                    a.wait_ge(pe_done, 3 + 2 * h)
                    nc.scalar.activation(wh_t[:, h % 2, :, :], pa[:, 0:C].unsqueeze(1).to_broadcast([P, 2, C]),
                                         ACT.Copy).then_inc(act_done, 1)
                    a.wait_ge(pe_done, 4 + 2 * h)
                    if h:
                        a.wait_ge(dve_done, h)
                    nc.scalar.activation(m_high[:], pb[:, 0:P], ACT.Copy).then_inc(act_done, 1)
                    nc.scalar.activation(m_split[0:C, h, :], pb[0:C, 0:P], ACT.Copy).then_inc(act_done, 1)
                a.wait_ge(dve_done, H + 1)
                nc.scalar.activation(std[:], deg[:], ACT.Sqrt, bias=ones[:, 0:1]).then_inc(act_done, 1)

            @block.tensor
            def _(pe):
                pe.wait_ge(loaded, 16 * SMALL)
                pe.wait_ge(ident_ok, 1)
                nc.tensor.transpose(pa[:, 0:C], w1_rows[:], ident[0:C, 0:C]).then_inc(pe_done, 1)
                nc.tensor.transpose(pb[:, 0:H], bh_rows[:], ident[0:H, 0:H]).then_inc(pe_done, 1)
                for h in range(H):
                    pe.wait_ge(act_done, 3 * (h + 1))
                    nc.tensor.transpose(pa[:, 0:C], wh_rows[:, h, :], ident[0:C, 0:C]).then_inc(pe_done, 1)
                    pe.wait_ge(act_done, 4 + 3 * h)
                    if h:
                        pe.wait_ge(dve_done, h)
                    pair = wh_t[:, h % 2, :, :].rearrange("p a c -> p (a c)")
                    nc.tensor.matmul(pb[:, 0:P], pair, pair, start=True, stop=True).then_inc(pe_done, 1)

            @block.vector
            def _(v):
                for h in range(H):
                    v.wait_ge(act_done, 6 + 3 * h)
                    nc.vector.tensor_tensor(m_split[C:P, h, :], pb[C:P, 0:P], m_high[C:P, :].bitcast(F32),
                                            ALU.subtract).then_inc(dve_done, 1)
                v.wait_ge(adj_in, 16 * T)
                nc.vector.tensor_reduce(deg[:], adjs[:], AX.X, ALU.add).then_inc(dve_done, 1)
                v.wait_ge(consts, 5)
                v.wait_ge(act_done, 4 + 3 * H)
                nc.vector.reciprocal(dinv[:], std[:]).then_inc(dve_done, 1)

        def layernorm(tag, high, low, scaled=None):
            with ExitStack() as ctx:
                square = sb(f"square{tag}", [P, T * B, C], ctx=ctx)
                mean = sb(f"mean{tag}", [P, T * B], ctx=ctx)
                total = sb(f"total{tag}", [P, T * B], ctx=ctx)
                var = sb(f"var{tag}", [P, T * B], ctx=ctx)
                dev = sb(f"dev{tag}", [P, T * B], ctx=ctx)
                rstd = sb(f"rstd{tag}", [P, T * B], ctx=ctx)
                steps, by_act = sems(ctx, f"ln_steps{tag}", f"ln_act{tag}")
                block = ctx.enter_context(nc.Block())
                rows = res[:].rearrange("p t b c -> p (t b) c")
                y = act[:].rearrange("p t b c -> p (t b) c")
                flat = (lambda t: t[:].rearrange("p t b c -> p (t b c)"))

                @block.scalar
                def _(a):
                    a.wait_ge(steps, 3)
                    nc.scalar.activation(square[:], y, ACT.Square).then_inc(by_act, 1)
                    a.wait_ge(steps, 4)
                    nc.scalar.activation(dev[:], var[:], ACT.Sqrt, scale=1.0 / C, bias=tiny[:, 0:1]).then_inc(by_act, 1)
                    if high is not None:
                        a.wait_ge(steps, 6)
                        src = act
                        if scaled is not None:
                            for t in range(T):
                                ins = nc.scalar.activation(scaled[:, t], act[:, t], ACT.Copy, scale=dinv[:, t:t + 1])
                            ins.then_inc(by_act, 1)
                            a.wait_ge(by_act, 3)
                            src = scaled
                        nc.scalar.activation(flat(high), flat(src), ACT.Copy).then_inc(by_act, 1)

                @block.vector
                def _(v):
                    done = Count(steps)
                    done.add(nc.vector.tensor_reduce(total[:], rows, AX.X, ALU.add))
                    v.wait_ge(steps, done.value)
                    done.add(nc.vector.tensor_scalar(mean[:], total[:], 1.0 / C, None, ALU.mult))
                    v.wait_ge(steps, done.value)
                    done.add(nc.vector.tensor_tensor(y, rows, mean[:].unsqueeze(2).to_broadcast([P, T * B, C]),
                                                     ALU.subtract))
                    v.wait_ge(by_act, 1)
                    done.add(nc.vector.tensor_reduce(var[:], square[:], AX.X, ALU.add))
                    v.wait_ge(by_act, 2)
                    done.add(nc.vector.reciprocal(rstd[:], dev[:]))
                    v.wait_ge(steps, done.value)
                    done.add(nc.vector.scalar_tensor_tensor(
                        out=y, in0=y, scalar=0.0, in1=rstd[:].unsqueeze(2).to_broadcast([P, T * B, C]),
                        op0=ALU.max, op1=ALU.mult))
                    if high is not None:
                        v.wait_ge(by_act, 3 if scaled is None else 4)
                        src = act if scaled is None else scaled
                        nc.vector.tensor_tensor(flat(low), flat(src), flat(high).bitcast(F32),
                                                ALU.subtract).then_inc(steps, 1)

        def graph_product(tag, v_high, v_low, finish):
            with ExitStack() as ctx:
                rows = sb(f"rows{tag}", [P, 2, N], ctx=ctx)
                cols_h = sb(f"cols_h{tag}", [P, 2, N], F32R, ctx=ctx)
                cols_l = sb(f"cols_l{tag}", [P, 2, N], F32R, ctx=ctx)
                turned = [ps(f"turned{tag}{k}", [P, HN], ctx) for k in range(4)]
                total = [ps(f"total_ps{tag}{k}", [P, BC], ctx) for k in range(2)]
                mixed = [ps(f"mixed{tag}{k}", [P, BC], ctx) for k in range(2)]
                staged, turned_ok, high_ok, low_ok, sum_ok, sum_used = sems(
                    ctx, f"staged{tag}", f"turned_ok{tag}", f"high_ok{tag}", f"low_ok{tag}", f"sum_ok{tag}",
                    f"sum_used{tag}")
                fin = finish(ctx, tag, total, mixed, sum_ok, sum_used, (staged, 2))
                block = ctx.enter_context(nc.Block())


                @block.tensor
                def _(pe):
                    with pe.Fori(0, T // 2) as i:
                        for u in range(2):
                            pe.wait_ge(staged, 2 * i + u + 1)
                            pe.wait_ge(low_ok, 2 * (2 * i + u))
                            for m in range(T):
                                ins = nc.tensor.transpose(turned[2 * u + m // 4][:, (m % 4) * P:(m % 4 + 1) * P],
                                                          rows[:, u, m * P:(m + 1) * P], ident[:])
                                if m % 4 == 3:
                                    ins.then_inc(turned_ok, 1)
                        for u in range(2):
                            pe.wait_ge(sum_used, 2 * i + u)
                            for half in range(2):
                                pe.wait_ge(low_ok, 2 * (2 * i + u) + half + 3)
                                for m in range(4 * half, 4 * half + 4):
                                    mt = slice(m * P, (m + 1) * P)
                                    vh = v_high[:, m].rearrange("p b c -> p (b c)")
                                    vl = v_low[:, m].rearrange("p b c -> p (b c)")
                                    nc.tensor.matmul(total[u][:], cols_h[:, u, mt], vh, start=(m == 0), stop=False)
                                    nc.tensor.matmul(total[u][:], cols_h[:, u, mt], vl, start=False, stop=False)
                                    ins = nc.tensor.matmul(total[u][:], cols_l[:, u, mt], vh, start=False,
                                                           stop=(m == T - 1))
                            ins.then_inc(sum_ok, 1)
                        for u in range(2):
                            fin.tensor(pe, i, u)

                @block.scalar
                def _(a):
                    for u in range(2):
                        nc.scalar.activation(rows[:, u, :], adjs[:, u, :], ACT.Copy).then_inc(staged, 1)
                    with a.Fori(0, T // 2) as i:
                        for u in range(2):
                            for half in range(2):
                                cs = slice(half * HN, (half + 1) * HN)
                                a.wait_ge(turned_ok, 2 * (2 * i + u) + half + 1)
                                nc.scalar.activation(cols_h[:, u, cs], turned[2 * u + half][:], ACT.Copy)\
                                    .then_inc(high_ok, 1)
                            nc.scalar.activation(rows[:, u, :], adjs[:, (2 * i + u + 2) % T, :], ACT.Copy)\
                                .then_inc(staged, 1)
                        for u in range(2):
                            fin.scalar(a, i, u)

                @block.vector
                def _(v):
                    nc.vector.memset(total[0][:, 0:1], 0.0).then_inc(sum_used, 1)
                    nc.vector.memset(total[0][:, 1:2], 0.0).then_inc(low_ok, 1)
                    nc.vector.memset(total[0][:, 2:3], 0.0).then_inc(low_ok, 1)
                    with v.Fori(0, T // 2) as i:
                        for u in range(2):
                            for half in range(2):
                                cs = slice(half * HN, (half + 1) * HN)
                                v.wait_ge(high_ok, 2 * (2 * i + u) + half + 1)
                                nc.vector.tensor_tensor(cols_l[:, u, cs], turned[2 * u + half][:],
                                                        cols_h[:, u, cs].bitcast(F32), ALU.subtract)\
                                    .then_inc(low_ok, 1)
                        for u in range(2):
                            fin.vector(v, i, u)

                if fin.sync:
                    @block.sync
                    def _(sp):
                        fin.sync(sp)

        def row(tile, t):
            return tile[:, t].rearrange("p b c -> p (b c)")

        class KeepSplit:
            sync = None

            def __init__(self, y, y_high, y_low):
                self.y, self.high, self.low = y, y_high, y_low

            def __call__(self, ctx, tag, total, mixed, sum_ok, sum_used, met):
                self.total, self.sum_ok, self.sum_used, self.met = total, sum_ok, sum_used, met
                self.split_ok, = sems(ctx, f"split_ok{tag}")
                return self

            def tensor(self, pe, i, u):
                pass

            def scalar(self, a, i, u):
                t = 2 * i + u
                wait_apart(a, self.sum_ok, t + 1, self.met)
                nc.scalar.activation(row(self.y, t), self.total[u][:], ACT.Copy)
                nc.scalar.activation(row(self.high, t), self.total[u][:], ACT.Copy).then_inc(self.split_ok, 1)

            def vector(self, v, i, u):
                t = 2 * i + u
                v.wait_ge(self.split_ok, t + 1)
                nc.vector.tensor_tensor(row(self.low, t), self.total[u][:], row(self.high, t).bitcast(F32),
                                        ALU.subtract).then_inc(self.sum_used, 1)

        class Chebyshev:
            sync = None

            def __init__(self, y, x):
                self.y, self.x = y, x

            def __call__(self, ctx, tag, total, mixed, sum_ok, sum_used, met):
                self.total, self.sum_ok, self.sum_used = total, sum_ok, sum_used
                return self

            def tensor(self, pe, i, u):
                pass

            def scalar(self, a, i, u):
                pass

            def vector(self, v, i, u):
                t = 2 * i + u
                v.wait_ge(self.sum_ok, t + 1)
                nc.vector.scalar_tensor_tensor(out=row(self.y, t), in0=self.total[u][:], scalar=2.0,
                                               in1=row(self.x, t), op0=ALU.mult, op1=ALU.subtract)\
                    .then_inc(self.sum_used, 1)

        class Mix:

            def __init__(self, weight, end, scaled=None, y_high=None, y_low=None):
                self.weight, self.end, self.scaled, self.high, self.low = weight, end, scaled, y_high, y_low
                self.sync = self.store if end == "store" else None

            def __call__(self, ctx, tag, total, mixed, sum_ok, sum_used, met):
                self.total, self.mixed, self.sum_ok, self.sum_used, self.met = total, mixed, sum_ok, sum_used, met
                self.node = sb(f"node{tag}", [P, 2, BC], ctx=ctx)
                self.feat = sb(f"feat{tag}", [P, 2, BC], ctx=ctx)
                self.last = sb(f"last{tag}", [P, 2, B, C], ctx=ctx)
                (self.node_ok, self.feat_ps, self.feat_ok, self.mix_ps, self.mix_used, self.last_ok, self.part,
                 self.stored) = sems(ctx, *(f"{n}{tag}" for n in (
                     "node_ok", "feat_ps", "feat_ok", "mix_ps", "mix_used", "last_ok", "part", "stored")))
                return self

            def tensor(self, pe, i, u):
                t = 2 * i + u
                if self.scaled is None:
                    pe.wait_ge(self.sum_used, t + 2)
                else:
                    pe.wait_ge(self.node_ok, t + 1)
                for k in range(4):
                    ks = slice(k * P, (k + 1) * P)
                    ins = nc.tensor.transpose(self.mixed[0][:, ks], self.node[:, u, ks], ident[:])
                ins.then_inc(self.feat_ps, 1)
                pe.wait_ge(self.feat_ok, t + 1)
                pe.wait_ge(self.mix_used, t)
                for k in range(4):
                    ks = slice(k * P, (k + 1) * P)
                    ins = nc.tensor.matmul(self.mixed[1][:, ks], self.feat[:, u, ks], self.weight, start=(k == 0),
                                           stop=(k == 3), skip_group_check=True)
                ins.then_inc(self.mix_ps, 1)

            def scalar(self, a, i, u):
                t = 2 * i + u
                if self.scaled is None:
                    a.wait_ge(self.sum_ok, t + 1)
                    nc.scalar.activation(self.node[:, u], self.total[u][:], ACT.Copy).then_inc(self.sum_used, 1)
                a.wait_ge(self.feat_ps, t + 1)
                nc.scalar.activation(self.feat[:, u], self.mixed[0][:], ACT.Copy).then_inc(self.feat_ok, 1)
                if self.end == "split":
                    if u == 0:
                        a.wait_ge(self.part, 2 * i)
                    a.wait_ge(self.mix_ps, t + 1)
                    nc.scalar.activation(self.last[:, u].rearrange("p b c -> p (b c)"), self.mixed[1][:],
                                         ACT.Relu).then_inc(self.mix_used, 1)
                    wait_apart(a, self.mix_used, t + 1, self.met)
                    nc.scalar.activation(row(self.high, t), self.last[:, u].rearrange("p b c -> p (b c)"),
                                         ACT.Copy).then_inc(self.last_ok, 1)

            def vector(self, v, i, u):
                t = 2 * i + u
                last = self.last[:, u].rearrange("p b c -> p (b c)")
                if self.scaled is not None:
                    v.wait_ge(self.sum_ok, t + 1)
                    nc.vector.tensor_tensor(self.feat_in(u), self.total[u][:], row(self.scaled, t), ALU.add)\
                        .then_inc(self.sum_used, 1)
                    v.wait_ge(self.sum_used, t + 2)
                    nc.vector.tensor_scalar(self.node[:, u], self.feat_in(u), dinv[:, bass.ds(t, 1)], None,
                                            ALU.mult).then_inc(self.node_ok, 1)
                if self.end == "split":
                    v.wait_ge(self.last_ok, t + 1)
                    nc.vector.tensor_tensor(row(self.low, t), last, row(self.high, t).bitcast(F32), ALU.subtract)\
                        .then_inc(self.part, 1)
                elif self.end == "residual":
                    v.wait_ge(self.mix_ps, t + 1)
                    nc.vector.tensor_tensor(row(res, t), row(res, t), self.mixed[1][:], ALU.add)\
                        .then_inc(self.mix_used, 1)
                else:
                    if u == 0:
                        v.wait_ge(self.stored, 32 * i)
                    v.wait_ge(self.mix_ps, t + 1)
                    nc.vector.scalar_tensor_tensor(out=last, in0=self.mixed[1][:], scalar=0.0, in1=row(res, t),
                                                   op0=ALU.max, op1=ALU.add).then_inc(self.mix_used, 1)

            def feat_in(self, u):
                return self.last[:, u].rearrange("p b c -> p (b c)")

            def store(self, sp):
                rows = out.rearrange("b (t p) c -> p t b c", p=P)
                with sp.Fori(0, T // 2) as i:
                    for u in range(2):
                        sp.wait_ge(self.mix_used, 2 * i + u + 1)
                        sp.dma_start(rows[:, 2 * i + u], self.last[:, u]).then_inc(self.stored, 16)
                sp.wait_ge(self.stored, 16 * T)

        def node_weights(y1, y2):
            with ExitStack() as ctx:
                w_a = sb("w_a", [P, D, O], ctx=ctx)
                w_b = sb("w_b", [C + 1, D, O], ctx=ctx)
                node_a = sb("node_a", [P, B, 2, C], ctx=ctx)
                node_b = sb("node_b", [P, B, C + 1], ctx=ctx)
                feat_a = sb("feat_a", [P, B, P], ctx=ctx)
                feat_b = sb("feat_b", [C + 1, B, P], ctx=ctx)
                emb_t = sb("emb_t", [P, D], ctx=ctx)
                acc = sb("acc", [P, B, O], ctx=ctx)
                turned_a = ps("turned_a", [P, B * P], ctx)
                turned_b = ps("turned_b", [P, B * P], ctx)
                prod = [ps(f"prod{k}", [P, 2, 512], ctx) for k in range(2)]
                w_in, staged, emb_ok, turned_ok, feat_ok, prod_ok, prod_used, steps, row_ok = sems(
                    ctx, "nw_in", "nw_staged", "nw_emb", "nw_turned", "nw_feat", "nw_prod", "nw_used", "nw_steps",
                    "nw_row")
                block = ctx.enter_context(nc.Block())
                DH = D // 2
                UNITS = B

                @block.sync
                def _(sp):
                    rows = l0_w.rearrange("d k i o -> (k i) d o")
                    sp.dma_start(w_a[:], rows[0:P]).then_inc(w_in, 16)
                    sp.dma_start(w_b[0:C], rows[P:P + C]).then_inc(w_in, 16)
                    sp.dma_start(w_b[C:C + 1], l0_b.unsqueeze(0)).then_inc(w_in, 16)
                    sp.wait_ge(w_in, 48)

                @block.scalar
                def _(a):
                    nc.scalar.activation(node_b[:, :, C:C + 1], ones[:, 0:B].unsqueeze(2), ACT.Copy)\
                        .then_inc(row_ok, 1)
                    with a.Fori(0, T) as t:
                        nc.scalar.activation(node_a[:, :, 0, :], act[:, t], ACT.Copy)
                        nc.scalar.activation(node_a[:, :, 1, :], y1[:, t], ACT.Copy)
                        nc.scalar.activation(node_b[:, :, 0:C], y2[:, t], ACT.Copy).then_inc(staged, 1)
                        wait_apart(a, prod_used, UNITS * t + 2, (row_ok, 1))
                        nc.scalar.activation(emb_t[:], emb_s[:, t], ACT.Copy).then_inc(emb_ok, 1)
                        for src, dst in ((turned_a, feat_a), (turned_b, feat_b)):
                            for half in range(2):
                                k = (src is turned_b) * 2 + half
                                a.wait_ge(turned_ok, 4 * t + k + 1)
                                n = dst.shape[0]
                                nc.scalar.activation(
                                    dst[:, 4 * half:4 * half + 4].rearrange("p b n -> p (b n)"),
                                    src[0:n, half * 512:(half + 1) * 512], ACT.Copy).then_inc(feat_ok, 1)

                @block.tensor
                def _(pe):
                    pe.wait_ge(w_in, 48)
                    with pe.Fori(0, T) as t:
                        pe.wait_ge(staged, t + 1)
                        for b in range(B):
                            ins = nc.tensor.transpose(turned_a[:, b * P:(b + 1) * P],
                                                      node_a[:, b].rearrange("p k c -> p (k c)"), ident[:])
                            if b % 4 == 3:
                                ins.then_inc(turned_ok, 1)
                        for b in range(B):
                            ins = nc.tensor.transpose(turned_b[0:C + 1, b * P:(b + 1) * P], node_b[:, b], ident[:])
                            if b % 4 == 3:
                                ins.then_inc(turned_ok, 1)
                        pe.wait_ge(feat_ok, 4 * t + 4)
                        for pair in range(4):
                            for half in range(2):
                                unit = 2 * pair + half
                                dh = slice(half * DH, (half + 1) * DH)
                                pe.wait_ge(prod_used, UNITS * t + unit + 1)
                                for k in range(2):
                                    b = 2 * pair + k
                                    nc.tensor.matmul(prod[half][:, k], feat_a[:, b],
                                                     w_a[:, dh].rearrange("p d o -> p (d o)"),
                                                     start=True, stop=False)
                                    ins = nc.tensor.matmul(prod[half][:, k], feat_b[:, b],
                                                           w_b[:, dh].rearrange("p d o -> p (d o)"),
                                                           start=False, stop=True)
                                ins.then_inc(prod_ok, 1)

                @block.vector
                def _(v):
                    nc.vector.memset(acc[:, 0, 0:1], 0.0).then_inc(prod_used, 1)
                    nc.vector.memset(acc[:, 0, 1:2], 0.0).then_inc(prod_used, 1)
                    v.wait_ge(prod_used, 2)
                    done = Count(steps)
                    with done.over(v, T, B * DH - UNITS) as t:
                        v.wait_ge(emb_ok, t + 1)
                        for pair in range(4):
                            bs = slice(2 * pair, 2 * pair + 2)
                            for half in range(2):
                                unit = 2 * pair + half
                                v.wait_ge(prod_ok, UNITS * t + unit + 1)
                                for d in range(DH):
                                    dd = half * DH + d
                                    if d:
                                        v.wait_ge(steps, done.value)
                                    elif half:
                                        v.wait_ge(prod_used, UNITS * t + unit + 2)
                                    ins = nc.vector.scalar_tensor_tensor(
                                        out=acc[:, bs] if dd < D - 1 else res[:, t, bs],
                                        in0=prod[half][:, :, d * O:(d + 1) * O],
                                        scalar=emb_t[:, dd:dd + 1], in1=acc[:, bs] if dd else res[:, t, bs],
                                        op0=ALU.mult, op1=ALU.add)
                                    if d < DH - 1:
                                        done.add(ins)
                                    else:
                                        ins.then_inc(prod_used, 1)

        class Attention:

            def __init__(self, ctx, tag, passes_in_flight):
                F = passes_in_flight
                self.u = sb(f"u{tag}", [P, F, N], F32R, ctx=ctx)
                self.xx_h = sb(f"xx_h{tag}", [P, F, N], F32R, ctx=ctx)
                self.xx_l = sb(f"xx_l{tag}", [P, F, N], F32R, ctx=ctx)
                self.values = sb(f"values{tag}", [P, T, C], ctx=ctx)
                self.score = sb(f"score{tag}", [P, 4, N], ctx=ctx)
                self.zero = sb(f"zero{tag}", [P, 2, N], ctx=ctx)
                self.prob_t = sb(f"prob_t{tag}", [P, 2, T, HN], ctx=ctx)
                self.low = sb(f"low{tag}", [P, F, T], ctx=ctx)
                self.sums = sb(f"sums{tag}", [P, F, T], ctx=ctx)
                self.rinv = sb(f"rinv{tag}", [P, F, T], ctx=ctx)
                self.s_ps = [ps(f"s_ps{tag}{k}", [P, N], ctx) for k in range(2)]
                self.turned = [ps(f"turned{tag}{k}", [P, HN], ctx) for k in range(2)]
                self.o_ps = ps(f"o_ps{tag}", [P, HN], ctx)
                self.misc = ps(f"misc{tag}", [P, HN], ctx)
                (self.s_ok, self.s_used, self.zero_ok, self.masked_ok, self.exp_ok, self.turned_ok,
                 self.turned_used, self.av_ok, self.av_used, self.rinv_ok, self.misc_ok, self.misc_used,
                 self.start_ok) = sems(ctx, *(f"{n}{tag}" for n in (
                     "s_ok", "s_used", "zero_ok", "masked_ok", "exp_ok", "turned_ok", "turned_used", "av_ok",
                     "av_used", "rinv_ok", "misc_ok", "misc_used", "start_ok")))

            def begin(self, v):
                nc.vector.memset(self.low[:], 0.0).then_inc(self.s_used, 1)
                nc.vector.memset(self.sums[:], 1.0).then_inc(self.turned_used, 1)
                nc.vector.memset(self.rinv[:], 1.0).then_inc(self.start_ok, 1)
                nc.vector.memset(self.zero[:, 0, 0:1], 0.0).then_inc(self.av_ok, 1)
                v.wait_ge(self.s_used, 1)
                v.wait_ge(self.turned_used, 1)
                v.wait_ge(self.start_ok, 1)

            def scores(self, pe, slot, xx, j, g):
                pe.wait_ge(self.s_used, g)
                rows = self.u[:, slot, j * P:(j + 1) * P]
                for half in range(2):
                    hs = slice(half * HN, (half + 1) * HN)
                    nc.tensor.matmul(self.s_ps[j % 2][:, hs], rows, self.xx_h[:, xx, hs], start=True, stop=False)
                    ins = nc.tensor.matmul(self.s_ps[j % 2][:, hs], rows, self.xx_l[:, xx, hs], start=False,
                                           stop=True)
                ins.then_inc(self.s_ok, 1)

            def turn(self, pe, j, g):
                pe.wait_ge(self.exp_ok, g + 1)
                for k in range(2):
                    pe.wait_ge(self.turned_used, 2 * g + k)
                    for m in range(4):
                        c = (4 * k + m) * P
                        ins = nc.tensor.transpose(self.turned[k][:, m * P:(m + 1) * P],
                                                  self.score[:, j % 4, c:c + P], ident[:])
                    ins.then_inc(self.turned_ok, 1)

            def mix_values(self, pe, half, p, between):
                pe.wait_ge(self.turned_used, 2 * (8 * p + 4 * half + 3) + 3)
                pe.wait_ge(self.av_used, 2 * p + half)
                for m in range(T):
                    ins = nc.tensor.matmul(self.o_ps[(m % 2) * C:(m % 2 + 1) * C, :], self.values[:, m, :],
                                           self.prob_t[:, half, m, :], start=(m < 2), stop=(m >= T - 2),
                                           skip_group_check=True)
                    if m == 3:
                        between()
                ins.then_inc(self.av_ok, 1)

            def multiply(self, v, j, g):
                v.wait_ge(self.s_ok, g + 1)
                nc.vector.tensor_tensor(self.score[:, j % 4, :], self.s_ps[j % 2][:], adjs[:, j, :], ALU.mult)\
                    .then_inc(self.s_used, 1)

            def find_zeros(self, v, j, g):
                v.wait_ge(self.s_used, g + 2)
                nc.vector.tensor_scalar(self.zero[:, j % 2, :], self.score[:, j % 4, :], 0.0, -NEG_INF,
                                        ALU.is_equal, ALU.mult).then_inc(self.zero_ok, 1)

            def mask(self, v, slot, j, g):
                wait_apart(v, self.zero_ok, g + 1, (self.av_ok, 1))
                nc.vector.tensor_tensor_reduce(self.score[:, j % 4, :], self.score[:, j % 4, :],
                                               self.zero[:, j % 2, :], 1.0, 3.0e38, ALU.add, ALU.min,
                                               self.low[:, slot, j:j + 1]).then_inc(self.masked_ok, 1)

            def invert(self, v, slot, half, p):
                v.wait_ge(self.exp_ok, 8 * p + 4 * half + 4)
                hs = slice(4 * half, 4 * half + 4)
                nc.vector.reciprocal(self.rinv[:, slot, hs], self.sums[:, slot, hs]).then_inc(self.rinv_ok, 1)

            def exponents(self, a, slot, j, g):
                a.wait_ge(self.masked_ok, g + 1)
                nc.scalar.activation(self.score[:, j % 4, :], self.score[:, j % 4, :], ACT.Exp, scale=-1.0,
                                     bias=self.low[:, slot, j:j + 1],
                                     accum_out=self.sums[:, slot, j:j + 1]).then_inc(self.exp_ok, 1)

            def keep_turned(self, a, j, g, p):
                for k in range(2):
                    if j % 4 == 0 and k == 0:
                        a.wait_ge(self.av_ok, 2 * p + j // 4)
                    a.wait_ge(self.turned_ok, 2 * g + k + 1)
                    nc.scalar.activation(
                        self.prob_t[:, j // 4, 4 * k:4 * k + 4, (j % 4) * P:(j % 4 + 1) * P],
                        self.turned[k][:].rearrange("p (m n) -> p m n", m=4), ACT.Copy)\
                        .then_inc(self.turned_used, 1)

        def heads():
            with ExitStack() as ctx:
                att = Attention(ctx, "h", 2)
                batch_x = sb("batch_x", [P, T, C], ctx=ctx)
                m_now = sb("m_now", [P, P], F32R, ctx=ctx)
                w_now = sb("w_now", [P, HID + 1], ctx=ctx)
                cat = sb("cat", [P, H, N], ctx=ctx)
                o_norm = sb("o_norm", [P, HN], ctx=ctx)
                recip = sb("recip", [P, HN], ctx=ctx)
                diag = sb("diag", [4, 4, P], ctx=ctx)
                biased = sb("biased", [P, HN], ctx=ctx)
                batch_ok, values_ok, m_ok, w_ok, xx_high, u_high, biased_ok, cat_ok = sems(
                    ctx, "batch_ok", "values_ok", "m_ok", "w_ok", "xx_high", "u_high", "biased_ok", "cat_ok")
                block = ctx.enter_context(nc.Block())
                misc, misc_ok, misc_used = att.misc, att.misc_ok, att.misc_used

                PER_BATCH = 2 + 8 * H + 1
                U0, U1, TURN, SPREAD, CAT = 0, 1, (2, 5), (3, 6), (4, 7)

                def base(b, i, s):
                    return 4 + PER_BATCH * b + 2 + 16 * i + 8 * s

                def xx_use(b):
                    return 4 + PER_BATCH * b

                def halves(k):
                    return slice(k * HN, (k + 1) * HN)

                def turn_x(pe, use, count):
                    pe.wait_ge(batch_ok, count)
                    for k in range(2):
                        pe.wait_ge(misc_used, use + k)
                        for m in range(4):
                            for side in range(2):
                                ins = nc.tensor.matmul(misc[side * C:(side + 1) * C, m * P:(m + 1) * P],
                                                       batch_x[:, 4 * k + m, :], ident[:], start=True, stop=True,
                                                       skip_group_check=True)
                        ins.then_inc(misc_ok, 1)

                def make_u(pe, use, k, xx, count):
                    pe.wait_ge(m_ok, count)
                    pe.wait_ge(misc_used, use)
                    nc.tensor.matmul(misc[:], m_now[:], att.xx_h[:, xx, halves(k)], start=True, stop=False)
                    nc.tensor.matmul(misc[:], m_now[:], att.xx_l[:, xx, halves(k)], start=False, stop=True)\
                        .then_inc(misc_ok, 1)

                @block.tensor
                def _(pe):
                    turn_x(pe, 0, 1)
                    for k in range(2):
                        make_u(pe, 2 + k, k, 0, 1)
                    pe.wait_ge(misc_used, 4)
                    for j in range(3):
                        att.scores(pe, 0, 0, j, j)
                    with pe.Fori(0, B) as b:
                        turn_x(pe, xx_use(b), b + 2)
                        with pe.Fori(0, H // 2) as i:
                            for s in range(2):
                                p = H * b + 2 * i + s
                                at = base(b, i, s)
                                xx = b % 2
                                xx_next = xx if s == 0 else ((4 * b + i + 1) // 4) % 2

                                def spread_turn(half):
                                    pe.wait_ge(att.rinv_ok, 2 * p + half + 1)
                                    pe.wait_ge(misc_used, at + TURN[half])
                                    nc.tensor.matmul(misc[0:4, 0:P], att.rinv[:, s, 4 * half:4 * half + 4], ident[:],
                                                     start=True, stop=True).then_inc(misc_ok, 1)

                                def spread(half):
                                    pe.wait_ge(misc_used, at + SPREAD[half])
                                    nc.tensor.matmul(misc[:], ones[0:4, :], diag[:].rearrange("q j n -> q (j n)"),
                                                     start=True, stop=True).then_inc(misc_ok, 1)

                                def head_out(half):
                                    pe.wait_ge(w_ok, p + 1)
                                    pe.wait_ge(misc_used, at + CAT[half])
                                    pe.wait_ge(att.av_used, 2 * p + half + 1)
                                    nc.tensor.matmul(misc[:], w_now[:, 0:HID], o_norm[:], start=True, stop=True)\
                                        .then_inc(misc_ok, 1)

                                for j in range(T):
                                    g = T * p + j
                                    att.turn(pe, j, g)
                                    if j in (1, 2):
                                        make_u(pe, at + j - 1, j - 1, xx_next, p + 2)
                                    if j == 4:
                                        head_out(0)
                                    if j == 5:
                                        pe.wait_ge(misc_used, at + U1 + 1)
                                    if j < 5:
                                        att.scores(pe, s, xx, j + 3, g + 3)
                                    else:
                                        att.scores(pe, 1 - s, xx_next, j - 5, g + 3)
                                    if j % 4 == 3:
                                        half = j // 4
                                        pe.wait_ge(values_ok, b + 1)
                                        att.mix_values(pe, half, p, lambda: spread_turn(half))
                                        spread(half)
                                head_out(1)
                        pe.wait_ge(cat_ok, 2 * H * (b + 1))
                        pe.wait_ge(misc_used, xx_use(b) + PER_BATCH - 1)
                        for h in range(H):
                            for k in range(2):
                                ins = nc.tensor.matmul(misc[k * C:(k + 1) * C, :], w_proj[:, h, :],
                                                       cat[:, h, halves(k)], start=(h == 0), stop=(h == H - 1),
                                                       skip_group_check=True)
                        ins.then_inc(misc_ok, 1)

                def u_part(a, use, slot, k):
                    a.wait_ge(misc_ok, use + 1)
                    nc.scalar.activation(att.u[:, slot, halves(k)], misc[:], ACT.Copy, scale=-1.0).then_inc(u_high, 1)

                @block.scalar
                def _(a):
                    for k in range(2):
                        a.wait_ge(misc_ok, k + 1)
                        nc.scalar.activation(att.xx_h[:, 0, halves(k)], misc[:], ACT.Copy).then_inc(xx_high, 1)
                    for k in range(2):
                        u_part(a, 2 + k, 0, k)
                    with a.Fori(0, B) as b:
                        for k in range(2):
                            wait_apart(a, misc_ok, xx_use(b) + k + 1, (att.start_ok, 1))
                            nc.scalar.activation(att.xx_h[:, (b + 1) % 2, halves(k)], misc[:], ACT.Copy)\
                                .then_inc(xx_high, 1)
                        with a.Fori(0, H // 2) as i:
                            for s in range(2):
                                p = H * b + 2 * i + s
                                at = base(b, i, s)

                                def copy_recip(half):
                                    a.wait_ge(misc_ok, at + SPREAD[half] + 1)
                                    nc.scalar.activation(recip[:], misc[:], ACT.Copy).then_inc(misc_used, 1)

                                def add_bias(half):
                                    a.wait_ge(cat_ok, 2 * p + half)
                                    a.wait_ge(misc_ok, at + CAT[half] + 1)
                                    nc.scalar.activation(biased[:], misc[:], ACT.Identity,
                                                         bias=w_now[:, HID:HID + 1]).then_inc(misc_used, 1)

                                for j in range(T):
                                    g = T * p + j
                                    att.exponents(a, s, j, g)
                                    if j == 5:
                                        copy_recip(0)
                                    if j:
                                        att.keep_turned(a, j - 1, g - 1, p)
                                    if j in (2, 3):
                                        u_part(a, at + j - 2, 1 - s, j - 2)
                                    if j == 5:
                                        add_bias(0)
                                att.keep_turned(a, T - 1, T * p + T - 1, p)
                                copy_recip(1)
                                add_bias(1)
                        wait_apart(a, misc_ok, xx_use(b) + PER_BATCH, (att.start_ok, 1))
                        nc.scalar.activation(act[:, :, b, :], misc[:].rearrange("p (t c) -> p t c", t=T), ACT.Copy)\
                            .then_inc(misc_used, 1)

                @block.gpsimd
                def _(pool):
                    pool.wait_ge(att.start_ok, 1)
                    nc.gpsimd.tensor_copy(batch_x[:], act[:, :, 0, :]).then_inc(batch_ok, 1)
                    nc.gpsimd.tensor_copy(m_now[:], m_split[:, 0, :]).then_inc(m_ok, 1)
                    nc.gpsimd.tensor_copy(w_now[:], w_cat[:, 0, :]).then_inc(w_ok, 1)
                    pool.wait_ge(misc_ok, 4)
                    nc.gpsimd.tensor_copy(m_now[:], m_split[:, 1, :]).then_inc(m_ok, 1)
                    with pool.Fori(0, B) as b:
                        wait_apart(pool, misc_used, xx_use(b), (att.start_ok, 1))
                        nc.gpsimd.tensor_copy(batch_x[:], act[:, :, (b + 1) % B, :]).then_inc(batch_ok, 1)
                        wait_apart(pool, att.av_ok, 2 * H * b + 1, (att.start_ok, 1))
                        nc.gpsimd.tensor_copy(att.values[:], act[:, :, b, :]).then_inc(values_ok, 1)
                        with pool.Fori(0, H // 2) as i:
                            for s in range(2):
                                at = base(b, i, s)
                                wait_apart(pool, misc_ok, at + TURN[0] + 1, (att.start_ok, 1))
                                nc.gpsimd.tensor_copy(m_now[:], m_split[:, (2 * i + s + 2) % H, :]).then_inc(m_ok, 1)
                                wait_apart(pool, misc_used, at + CAT[1] + 1, (att.start_ok, 1))
                                nc.gpsimd.tensor_copy(w_now[:], w_cat[:, (2 * i + s + 1) % H, :]).then_inc(w_ok, 1)

                def u_low(v, count, slot, k):
                    v.wait_ge(u_high, count)
                    nc.vector.scalar_tensor_tensor(out=att.u[C:P, slot, halves(k)], in0=misc[C:P, :], scalar=-1.0,
                                                   in1=att.u[C:P, slot, halves(k)].bitcast(F32), op0=ALU.mult,
                                                   op1=ALU.subtract).then_inc(misc_used, 1)

                def tile(v, s, j, g):
                    att.multiply(v, j, g)
                    att.find_zeros(v, j, g)
                    att.mask(v, s, j, g)

                @block.vector
                def _(v):
                    att.begin(v)
                    for k in range(2):
                        v.wait_ge(xx_high, k + 1)
                        nc.vector.tensor_tensor(att.xx_l[:, 0, halves(k)], misc[:],
                                                att.xx_h[:, 0, halves(k)].bitcast(F32), ALU.subtract)\
                            .then_inc(misc_used, 1)
                    for k in range(2):
                        u_low(v, k + 1, 0, k)
                    for j in range(2):
                        tile(v, 0, j, j)
                    with v.Fori(0, B) as b:
                        for k in range(2):
                            v.wait_ge(xx_high, 2 * b + k + 3)
                            nc.vector.tensor_tensor(att.xx_l[:, (b + 1) % 2, halves(k)], misc[:],
                                                    att.xx_h[:, (b + 1) % 2, halves(k)].bitcast(F32), ALU.subtract)\
                                .then_inc(misc_used, 1)
                        with v.Fori(0, H // 2) as i:
                            for s in range(2):
                                p = H * b + 2 * i + s
                                at = base(b, i, s)

                                def make_diag(half):
                                    v.wait_ge(misc_ok, at + TURN[half] + 1)
                                    nc.vector.tensor_tensor(
                                        diag[:], misc[0:4, 0:P].unsqueeze(1).to_broadcast([4, 4, P]),
                                        ident[0:4, 0:4].unsqueeze(2).to_broadcast([4, 4, P]), ALU.mult)\
                                        .then_inc(misc_used, 1)

                                def normalise(half):
                                    v.wait_ge(att.av_ok, 2 * p + half + 2)
                                    v.wait_ge(misc_used, at + SPREAD[half] + 1)
                                    nc.vector.tensor_tensor(o_norm[:], att.o_ps[:], recip[:], ALU.mult)\
                                        .then_inc(att.av_used, 1)

                                def leaky(half):
                                    v.wait_ge(misc_used, at + CAT[half] + 1)
                                    nc.vector.scalar_tensor_tensor(
                                        out=cat[:, 2 * i + s, halves(half)], in0=biased[:], scalar=SLOPE,
                                        in1=biased[:], op0=ALU.mult, op1=ALU.max).then_inc(cat_ok, 1)

                                for j in range(2, T + 2):
                                    tile(v, s if j < T else 1 - s, j % T, T * p + j)
                                    if j in (4, 5):
                                        u_low(v, 2 * p + j - 1, 1 - s, j - 4)
                                    if j in (4, 8):
                                        att.invert(v, s, j // 4 - 1, p)
                                    if j in (6, 9):
                                        half = j // 8
                                        make_diag(half)
                                        normalise(half)
                                    if j == 7:
                                        leaky(0)
                                leaky(1)

        def output_attention():
            with ExitStack() as ctx:
                att = Attention(ctx, "o", 1)
                g_now = sb("g_now", [P, HN], ctx=ctx)
                o_sb = sb("o_sb", [P, HN], ctx=ctx)
                y = sb("y", [P, 2, 4, C], ctx=ctx)
                y_leaky = sb("y_leaky", [P, 2, 4, C], ctx=ctx)
                g_ok, xx_high, u_ok, o_copied, y_steps, res_ok = sems(
                    ctx, "g_ok", "xx_high_o", "u_ok", "o_copied", "y_steps", "res_ok")
                block = ctx.enter_context(nc.Block())
                misc, misc_ok, misc_used = att.misc, att.misc_ok, att.misc_used
                PER_PASS = 5

                def halves(k):
                    return slice(k * HN, (k + 1) * HN)

                @block.gpsimd
                def _(pool):
                    pool.wait_ge(att.start_ok, 1)
                    with pool.Fori(0, B) as p:
                        wait_apart(pool, misc_used, PER_PASS * p, (att.start_ok, 1))
                        nc.gpsimd.tensor_copy(g_now[:].rearrange("p (t c) -> p t c", t=T), act[:, :, p, :])\
                            .then_inc(g_ok, 1)

                @block.tensor
                def _(pe):
                    with pe.Fori(0, B) as p:
                        at = PER_PASS * p
                        pe.wait_ge(g_ok, p + 1)
                        for k in range(2):
                            pe.wait_ge(misc_used, at + k)
                            nc.tensor.matmul(misc[:], fold[k * C:(k + 1) * C, :], g_now[k * C:(k + 1) * C, :],
                                             start=True, stop=True).then_inc(misc_ok, 1)
                        pe.wait_ge(misc_used, at + 2)
                        for m in range(4):
                            ins = nc.tensor.transpose(misc[:, m * P:(m + 1) * P], g_now[:, m * P:(m + 1) * P],
                                                      ident[:])
                        ins.then_inc(misc_ok, 1)
                        pe.wait_ge(u_ok, 2 * p + 2)
                        for j in range(2):
                            att.scores(pe, 0, 0, j, T * p + j)
                        for j in range(T):
                            g = T * p + j
                            att.turn(pe, j, g)
                            if j + 2 < T:
                                att.scores(pe, 0, 0, j + 2, g + 2)
                            if j % 4 == 3:
                                half = j // 4
                                pe.wait_ge(misc_used, at + 3)
                                att.mix_values(pe, half, p, lambda: None)
                                pe.wait_ge(misc_used, at + 3 + half)
                                pe.wait_ge(att.av_used, 2 * p + half + 1)
                                for m in range(4):
                                    ins = nc.tensor.matmul(misc[:, m * C:(m + 1) * C], o_sb[:, m * P:(m + 1) * P],
                                                           fold[:, 0:C], start=True, stop=True,
                                                           skip_group_check=True)
                                ins.then_inc(misc_ok, 1)

                def copy_out(a, p, half):
                    a.wait_ge(att.av_ok, 2 * p + half + 2)
                    nc.scalar.activation(o_sb[:], att.o_ps[:], ACT.Copy).then_inc(att.av_used, 1)

                @block.scalar
                def _(a):
                    with a.Fori(0, B) as p:
                        at = PER_PASS * p
                        for k in range(2):
                            a.wait_ge(misc_ok, at + k + 1)
                            nc.scalar.activation(att.xx_h[:, 0, halves(k)], misc[:], ACT.Copy).then_inc(xx_high, 1)
                        a.wait_ge(misc_ok, at + 3)
                        nc.scalar.activation(att.values[:].rearrange("p (a m) c -> p m a c", a=2),
                                             misc[:].rearrange("p (m a c) -> p m a c", m=4, a=2),
                                             ACT.Copy).then_inc(misc_used, 1)
                        for j in range(T):
                            g = T * p + j
                            att.exponents(a, 0, j, g)
                            if j == 5:
                                copy_out(a, p, 0)
                            if j:
                                att.keep_turned(a, j - 1, g - 1, p)
                        att.keep_turned(a, T - 1, T * p + T - 1, p)
                        copy_out(a, p, 1)

                @block.vector
                def _(v):
                    att.begin(v)
                    steps = Count(y_steps)
                    with steps.over(v, B, 10) as p:
                        at = PER_PASS * p

                        def finish(half):
                            att.invert(v, 0, half, p)
                            v.wait_ge(misc_ok, at + 4 + half)
                            v.wait_ge(att.rinv_ok, 2 * p + half + 1)
                            for m in range(4):
                                ins = nc.vector.scalar_tensor_tensor(
                                    out=y[:, half, m], in0=misc[:, m * C:(m + 1) * C],
                                    scalar=att.rinv[:, 0, 4 * half + m:4 * half + m + 1], in1=b_proj[:],
                                    op0=ALU.mult, op1=ALU.add)
                                if m < 3:
                                    steps.add(ins)
                                else:
                                    ins.then_inc(misc_used, 1)
                            v.wait_ge(misc_used, at + 4 + half)
                            steps.add(nc.vector.scalar_tensor_tensor(
                                out=y_leaky[:, half], in0=y[:, half], scalar=SLOPE, in1=y[:, half],
                                op0=ALU.mult, op1=ALU.max))
                            v.wait_ge(y_steps, steps.value)
                            ts = slice(4 * half, 4 * half + 4)
                            steps.add(nc.vector.tensor_tensor(res[:, ts, p], res[:, ts, p], y_leaky[:, half],
                                                              ALU.add))

                        for k in range(2):
                            v.wait_ge(xx_high, 2 * p + k + 1)
                            nc.vector.tensor_tensor(att.xx_l[:, 0, halves(k)], misc[:],
                                                    att.xx_h[:, 0, halves(k)].bitcast(F32), ALU.subtract)\
                                .then_inc(misc_used, 1)
                        v.wait_ge(misc_used, at + 2)
                        for part, rows in ((att.xx_h, slice(0, C)), (att.xx_l, slice(C, P))):
                            nc.vector.tensor_scalar(att.u[rows, 0, :], part[rows, 0, :].bitcast(F32), -1.0, None,
                                                    ALU.mult).then_inc(u_ok, 1)
                        for j in range(T):
                            g = T * p + j
                            att.multiply(v, j, g)
                            att.find_zeros(v, j, g)
                            att.mask(v, 0, j, g)
                            if j == 5:
                                finish(0)
                        finish(1)

        def split_tiles(ctx, *names):
            return [sb(n, [P, T, B, C], F32R, ctx=ctx) for n in names]

        with ExitStack() as ctx:
            high, low = split_tiles(ctx, "high", "low")
            y1 = sb("y1", [P, T, B, C], ctx=ctx)
            with ExitStack() as layer0:
                y_high, y_low = split_tiles(layer0, "y1_high", "y1_low")
                y2 = sb("y2", [P, T, B, C], ctx=layer0)
                layernorm("0", high, low)
                graph_product("0", high, low, KeepSplit(y1, y_high, y_low))
                graph_product("1", y_high, y_low, Chebyshev(y2, act))
                node_weights(y1, y2)
            layernorm("1", high, low, scaled=y1)
            graph_product("2", high, low, Mix(bd1[:], "residual", scaled=y1))
            layernorm("2", None, None)
        heads()
        output_attention()
        with ExitStack() as ctx:
            high, low, y_high, y_low = split_tiles(ctx, "high3", "low3", "y_high3", "y_low3")
            layernorm("3", high, low)
            graph_product("3", high, low, Mix(bd3[:, 0], "split", y_high=y_high, y_low=y_low))
            graph_product("4", y_high, y_low, Mix(bd3[:, 1], "store"))


_INS = ["x", "adj", "L0_gnn_embedding", "L0_gnn_weight", "L0_gnn_bias", "L1_gnn_W", "L2_gnn_Wh", "L2_gnn_bh",
        "L2_gnn_W_out", "L2_gnn_b_out", "L3_gnn_net_params"]


def kernel(**inputs):
    import numpy as _np
    import concourse.bacc as _bacc
    from concourse.bass_utils import run_bass_kernel_spmd as _run

    nc = _bacc.Bacc("TRN2", target_bir_lowering=False, num_devices=1)
    arrays, args = {}, []
    for name in _INS:
        a = _np.ascontiguousarray(inputs[name])
        arrays[f"in_{name}"] = a
        args.append(nc.dram_tensor(f"in_{name}", a.shape, mybir.dt.from_np(a.dtype), kind="ExternalInput").ap())
    out = nc.dram_tensor("out", inputs["x"].shape, F32, kind="ExternalOutput").ap()
    build_kernel(nc, *args, out)
    return _run(nc, [arrays], core_ids=[0]).results[0]["out"]
```

```python
from contextlib import ExitStack, contextmanager

import concourse.bass as bass
from concourse import mybir

F32 = mybir.dt.float32
F32R = mybir.dt.float32r
ALU = mybir.AluOpType
ACT = mybir.ActivationFunctionType
AX = mybir.AxisListType

P = 128
NEG_INF = -1e16
EPS = 1e-5
SLOPE = 0.01


def wait_apart(eng, sem, value):
    eng.wait_ge(sem, value)
    eng.nop(nofuse=True)


class Count:

    def __init__(self, sem):
        self.sem, self.value = sem, 0

    def add(self, instruction):
        instruction.then_inc(self.sem, 1)
        self.value = self.value + 1

    @contextmanager
    def over(self, eng, trips, each):
        start = self.value
        with eng.Fori(0, trips) as i:
            self.value = start + i * each
            yield i
        self.value = start + trips * each


def build_kernel(nc, x, adj, emb, l0_w, l0_b, l1_w, wh, bh, w_out, b_out, l3_w, out):
    B, N, C = x.shape
    D, K, _, O = l0_w.shape
    H, _, HID = wh.shape
    T = N // P
    BC = B * C
    HN = N // 2
    G2 = 2 * C
    assert BC == HN == 512 and G2 == P and HID == P and K == 3

    with ExitStack() as whole:
        def sb(name, shape, dt=F32, ctx=whole):
            return ctx.enter_context(nc.sbuf_tensor(name, shape, dt))

        def ps(name, shape, ctx=whole):
            return ctx.enter_context(nc.psum_tensor(name, shape, F32))

        adjs = sb("adjs", [P, T, N])
        res = sb("res", [P, T, B, C])
        act = sb("act", [P, T, B, C])
        emb_s = sb("emb_s", [P, T, D])
        ident = sb("ident", [P, P])
        fold = sb("fold", [P, P])
        ones = sb("ones", [P, P])
        dinv = sb("dinv", [P, T])
        bd1 = sb("bd1", [P, P])
        bd3 = sb("bd3", [P, 2, P])
        w_heads = sb("w_heads", [P, H, HID + 1 + O])
        m_split = sb("m_split", [P, H, P], F32R)
        b_proj = sb("b_proj", [P, O])
        tiny = sb("tiny", [P, 2])

        def sems(ctx, *names):
            return [ctx.enter_context(nc.semaphore(n)) for n in names]

        def split_halves(ap):
            return ap.rearrange("p (t x) -> p t x", t=2)

        with ExitStack() as ctx:
            w1_rows = sb("w1_rows", [C, 2, C], ctx=ctx)
            wh_rows = sb("wh_rows", [C, H, HID], ctx=ctx)
            bh_rows = sb("bh_rows", [H, HID], ctx=ctx)
            wh_t = sb("wh_t", [P, 2, 2, C], ctx=ctx)
            m_high = sb("m_high", [P, P], F32R, ctx=ctx)
            deg = sb("deg", [P, T], ctx=ctx)
            std = sb("std", [P, T], ctx=ctx)
            pa = ps("pa", [P, 512], ctx)
            pb = ps("pb", [P, 512], ctx)
            loaded, adj_in, zeroed, ident_ok, consts, pe_done, act_done, dve_done = sems(
                ctx, "loaded", "adj_in", "zeroed", "ident_ok", "consts", "prep_pe", "prep_act", "prep_dve")
            block = ctx.enter_context(nc.Block())
            SMALL = 13 + T

            @block.sync
            def _(sp):
                for t in range(T):
                    sp.dma_start(res[:, t], x.rearrange("b (t p) c -> t p b c", p=P)[t]).then_inc(loaded, 16)
                for t in range(T):
                    sp.dma_start(adjs[:, t, :], adj[t * P:(t + 1) * P, :]).then_inc(adj_in, 16)
                sp.wait_ge(adj_in, 16 * T)
                sp.wait_ge(loaded, 16 * SMALL)

            @block.gpsimd
            def _(pool):
                for tile in (ident, fold, bd1, bd3):
                    nc.gpsimd.memset(tile[:], 0.0).then_inc(zeroed, 1)
                nc.gpsimd.memset(ones[:], 1.0).then_inc(consts, 1)
                nc.gpsimd.memset(tiny[:], EPS).then_inc(consts, 1)
                pool.wait_ge(zeroed, 4)
                nc.gpsimd.affine_select(out=ident[:], in_=ident[:], compare_op=ALU.not_equal, fill=1.0, base=0,
                                        pattern=[[-1, P]], channel_multiplier=1).then_inc(ident_ok, 1)
                for n, base in enumerate((0, C, -C)):
                    if n:
                        pool.wait_ge(consts, 2 + n)
                    nc.gpsimd.affine_select(out=fold[:], in_=fold[:], compare_op=ALU.not_equal, fill=1.0,
                                            base=base, pattern=[[-1, P]], channel_multiplier=1).then_inc(consts, 1)

            @block.scalar
            def _(a):
                a.dma_start(emb_s[:], emb.rearrange("(t p) d -> p t d", p=P)).then_inc(loaded, 16)
                for k in range(2):
                    a.dma_start(w1_rows[:, k, :], l1_w).then_inc(loaded, 16)
                a.dma_start(wh_rows[:], wh.rearrange("h c d -> c h d")).then_inc(loaded, 16)
                a.dma_start(bh_rows[:], bh).then_inc(loaded, 16)
                for k in range(2):
                    a.dma_start(w_heads[k * C:(k + 1) * C, :, 0:HID], wh.rearrange("h c d -> c h d")).then_inc(loaded, 16)
                a.dma_start(w_heads[:, :, HID + 1:], w_out.rearrange("(h d) o -> d h o", d=P)).then_inc(loaded, 16)
                a.dma_start(b_proj[:], b_out.partition_broadcast(P)).then_inc(loaded, 16)
                a.wait_ge(zeroed, 4)
                for layer in range(2):
                    for k in range(2):
                        a.dma_start(bd3[k * C:(k + 1) * C, layer, k * C:(k + 1) * C],
                                    l3_w.rearrange("(l f g) -> l f g", l=2, f=C)[layer]).then_inc(loaded, 16)
                a.wait_ge(pe_done, 1)
                for k in range(2):
                    nc.scalar.activation(bd1[k * C:(k + 1) * C, k * C:(k + 1) * C],
                                         pa[k * C:(k + 1) * C, 0:C], ACT.Copy).then_inc(act_done, 1)
                a.wait_ge(pe_done, 2)
                nc.scalar.activation(w_heads[:, :, HID], pb[:, 0:H], ACT.Copy).then_inc(act_done, 1)
                for h in range(H):
                    a.wait_ge(pe_done, 3 + 2 * h)
                    nc.scalar.activation(wh_t[:, h % 2, :, :], pa[:, 0:C].unsqueeze(1).to_broadcast([P, 2, C]),
                                         ACT.Copy).then_inc(act_done, 1)
                    a.wait_ge(pe_done, 4 + 2 * h)
                    if h:
                        a.wait_ge(dve_done, h)
                    nc.scalar.activation(m_high[:], pb[:, 0:P], ACT.Copy).then_inc(act_done, 1)
                    nc.scalar.activation(m_split[0:C, h, :], pb[0:C, 0:P], ACT.Copy).then_inc(act_done, 1)
                a.wait_ge(dve_done, H + 1)
                nc.scalar.activation(std[:], deg[:], ACT.Sqrt, bias=ones[:, 0:1]).then_inc(act_done, 1)

            @block.tensor
            def _(pe):
                pe.wait_ge(loaded, 16 * SMALL)
                pe.wait_ge(ident_ok, 1)
                nc.tensor.transpose(pa[:, 0:C], w1_rows[:], ident[0:C, 0:C]).then_inc(pe_done, 1)
                nc.tensor.transpose(pb[:, 0:H], bh_rows[:], ident[0:H, 0:H]).then_inc(pe_done, 1)
                for h in range(H):
                    pe.wait_ge(act_done, 3 * (h + 1))
                    nc.tensor.transpose(pa[:, 0:C], wh_rows[:, h, :], ident[0:C, 0:C]).then_inc(pe_done, 1)
                    pe.wait_ge(act_done, 4 + 3 * h)
                    if h:
                        pe.wait_ge(dve_done, h)
                    pair = wh_t[:, h % 2, :, :].rearrange("p a c -> p (a c)")
                    nc.tensor.matmul(pb[:, 0:P], pair, pair, start=True, stop=True).then_inc(pe_done, 1)

            @block.vector
            def _(v):
                for h in range(H):
                    v.wait_ge(act_done, 6 + 3 * h)
                    nc.vector.tensor_tensor(m_split[C:P, h, :], pb[C:P, 0:P], m_high[C:P, :].bitcast(F32),
                                            ALU.subtract).then_inc(dve_done, 1)
                v.wait_ge(adj_in, 16 * T)
                nc.vector.tensor_reduce(deg[:], adjs[:], AX.X, ALU.add).then_inc(dve_done, 1)
                v.wait_ge(consts, 5)
                v.wait_ge(act_done, 4 + 3 * H)
                nc.vector.reciprocal(dinv[:], std[:]).then_inc(dve_done, 1)

        def layernorm(tag, high, low, scaled=None):
            with ExitStack() as ctx:
                square = sb(f"square{tag}", [P, T * B, C], ctx=ctx)
                mean = sb(f"mean{tag}", [P, T * B], ctx=ctx)
                total = sb(f"total{tag}", [P, T * B], ctx=ctx)
                var = sb(f"var{tag}", [P, T * B], ctx=ctx)
                dev = sb(f"dev{tag}", [P, T * B], ctx=ctx)
                rstd = sb(f"rstd{tag}", [P, T * B], ctx=ctx)
                steps, by_act = sems(ctx, f"ln_steps{tag}", f"ln_act{tag}")
                block = ctx.enter_context(nc.Block())
                rows = res[:].rearrange("p t b c -> p (t b) c")
                y = act[:].rearrange("p t b c -> p (t b) c")
                flat = (lambda t: t[:].rearrange("p t b c -> p (t b c)"))

                @block.scalar
                def _(a):
                    a.wait_ge(steps, 3)
                    nc.scalar.activation(square[:], y, ACT.Square).then_inc(by_act, 1)
                    a.wait_ge(steps, 4)
                    nc.scalar.activation(dev[:], var[:], ACT.Sqrt, scale=1.0 / C, bias=tiny[:, 0:1]).then_inc(by_act, 1)
                    if high is not None:
                        a.wait_ge(steps, 6)
                        src = act
                        if scaled is not None:
                            for t in range(T):
                                ins = nc.scalar.activation(scaled[:, t], act[:, t], ACT.Copy, scale=dinv[:, t:t + 1])
                            ins.then_inc(by_act, 1)
                            a.wait_ge(by_act, 3)
                            src = scaled
                        nc.scalar.activation(flat(high), flat(src), ACT.Copy).then_inc(by_act, 1)

                @block.vector
                def _(v):
                    done = Count(steps)
                    done.add(nc.vector.tensor_reduce(total[:], rows, AX.X, ALU.add))
                    v.wait_ge(steps, done.value)
                    done.add(nc.vector.tensor_scalar(mean[:], total[:], 1.0 / C, None, ALU.mult))
                    v.wait_ge(steps, done.value)
                    done.add(nc.vector.tensor_tensor(y, rows, mean[:].unsqueeze(2).to_broadcast([P, T * B, C]),
                                                     ALU.subtract))
                    v.wait_ge(by_act, 1)
                    done.add(nc.vector.tensor_reduce(var[:], square[:], AX.X, ALU.add))
                    v.wait_ge(by_act, 2)
                    done.add(nc.vector.reciprocal(rstd[:], dev[:]))
                    v.wait_ge(steps, done.value)
                    done.add(nc.vector.scalar_tensor_tensor(
                        out=y, in0=y, scalar=0.0, in1=rstd[:].unsqueeze(2).to_broadcast([P, T * B, C]),
                        op0=ALU.max, op1=ALU.mult))
                    if high is not None:
                        v.wait_ge(by_act, 3 if scaled is None else 4)
                        src = act if scaled is None else scaled
                        nc.vector.tensor_tensor(flat(low), flat(src), flat(high).bitcast(F32),
                                                ALU.subtract).then_inc(steps, 1)

        def graph_product(tag, v_high, v_low, finish):
            with ExitStack() as ctx:
                rows = sb(f"rows{tag}", [P, 2, N], ctx=ctx)
                cols_h = sb(f"cols_h{tag}", [P, 2, N], F32R, ctx=ctx)
                cols_l = sb(f"cols_l{tag}", [P, 2, N], F32R, ctx=ctx)
                turned = [ps(f"turned{tag}{k}", [P, HN], ctx) for k in range(4)]
                total = [ps(f"total_ps{tag}{k}", [P, BC], ctx) for k in range(2)]
                mixed = [ps(f"mixed{tag}{k}", [P, BC], ctx) for k in range(2)]
                staged, turned_ok, high_ok, low_ok, sum_ok, sum_used = sems(
                    ctx, f"staged{tag}", f"turned_ok{tag}", f"high_ok{tag}", f"low_ok{tag}", f"sum_ok{tag}",
                    f"sum_used{tag}")
                fin = finish(ctx, tag, total, mixed, sum_ok, sum_used)
                block = ctx.enter_context(nc.Block())


                @block.tensor
                def _(pe):
                    with pe.Fori(0, T // 2) as i:
                        for u in range(2):
                            pe.wait_ge(staged, 2 * i + u + 1)
                            pe.wait_ge(low_ok, 2 * (2 * i + u))
                            for m in range(T):
                                ins = nc.tensor.transpose(turned[2 * u + m // 4][:, (m % 4) * P:(m % 4 + 1) * P],
                                                          rows[:, u, m * P:(m + 1) * P], ident[:])
                                if m % 4 == 3:
                                    ins.then_inc(turned_ok, 1)
                        for u in range(2):
                            pe.wait_ge(sum_used, 2 * i + u)
                            for half in range(2):
                                pe.wait_ge(low_ok, 2 * (2 * i + u) + half + 3)
                                for m in range(4 * half, 4 * half + 4):
                                    mt = slice(m * P, (m + 1) * P)
                                    vh = v_high[:, m].rearrange("p b c -> p (b c)")
                                    vl = v_low[:, m].rearrange("p b c -> p (b c)")
                                    nc.tensor.matmul(total[u][:], cols_h[:, u, mt], vh, start=(m == 0), stop=False)
                                    nc.tensor.matmul(total[u][:], cols_h[:, u, mt], vl, start=False, stop=False)
                                    ins = nc.tensor.matmul(total[u][:], cols_l[:, u, mt], vh, start=False,
                                                           stop=(m == T - 1))
                            ins.then_inc(sum_ok, 1)
                        for u in range(2):
                            fin.tensor(pe, i, u)

                @block.scalar
                def _(a):
                    for u in range(2):
                        nc.scalar.activation(rows[:, u, :], adjs[:, u, :], ACT.Copy).then_inc(staged, 1)
                    with a.Fori(0, T // 2) as i:
                        for u in range(2):
                            for half in range(2):
                                cs = slice(half * HN, (half + 1) * HN)
                                a.wait_ge(turned_ok, 2 * (2 * i + u) + half + 1)
                                nc.scalar.activation(cols_h[:, u, cs], turned[2 * u + half][:], ACT.Copy)\
                                    .then_inc(high_ok, 1)
                            nc.scalar.activation(rows[:, u, :], adjs[:, (2 * i + u + 2) % T, :], ACT.Copy)\
                                .then_inc(staged, 1)
                        for u in range(2):
                            fin.scalar(a, i, u)

                @block.vector
                def _(v):
                    nc.vector.memset(total[0][:, 0:1], 0.0).then_inc(sum_used, 1)
                    nc.vector.memset(total[0][:, 1:2], 0.0).then_inc(low_ok, 1)
                    nc.vector.memset(total[0][:, 2:3], 0.0).then_inc(low_ok, 1)
                    with v.Fori(0, T // 2) as i:
                        for u in range(2):
                            for half in range(2):
                                cs = slice(half * HN, (half + 1) * HN)
                                v.wait_ge(high_ok, 2 * (2 * i + u) + half + 1)
                                nc.vector.tensor_tensor(cols_l[:, u, cs], turned[2 * u + half][:],
                                                        cols_h[:, u, cs].bitcast(F32), ALU.subtract)\
                                    .then_inc(low_ok, 1)
                        for u in range(2):
                            fin.vector(v, i, u)

                if fin.sync:
                    @block.sync
                    def _(sp):
                        fin.sync(sp)

        def row(tile, t):
            return tile[:, t].rearrange("p b c -> p (b c)")

        class KeepSplit:
            sync = None

            def __init__(self, y, y_high, y_low):
                self.y, self.high, self.low = y, y_high, y_low

            def __call__(self, ctx, tag, total, mixed, sum_ok, sum_used):
                self.total, self.sum_ok, self.sum_used = total, sum_ok, sum_used
                self.split_ok, = sems(ctx, f"split_ok{tag}")
                return self

            def tensor(self, pe, i, u):
                pass

            def scalar(self, a, i, u):
                t = 2 * i + u
                wait_apart(a, self.sum_ok, t + 1)
                nc.scalar.activation(row(self.y, t), self.total[u][:], ACT.Copy)
                nc.scalar.activation(row(self.high, t), self.total[u][:], ACT.Copy).then_inc(self.split_ok, 1)

            def vector(self, v, i, u):
                t = 2 * i + u
                v.wait_ge(self.split_ok, t + 1)
                nc.vector.tensor_tensor(row(self.low, t), self.total[u][:], row(self.high, t).bitcast(F32),
                                        ALU.subtract).then_inc(self.sum_used, 1)

        class Chebyshev:
            sync = None

            def __init__(self, y, x):
                self.y, self.x = y, x

            def __call__(self, ctx, tag, total, mixed, sum_ok, sum_used):
                self.total, self.sum_ok, self.sum_used = total, sum_ok, sum_used
                return self

            def tensor(self, pe, i, u):
                pass

            def scalar(self, a, i, u):
                pass

            def vector(self, v, i, u):
                t = 2 * i + u
                v.wait_ge(self.sum_ok, t + 1)
                nc.vector.scalar_tensor_tensor(out=row(self.y, t), in0=self.total[u][:], scalar=2.0,
                                               in1=row(self.x, t), op0=ALU.mult, op1=ALU.subtract)\
                    .then_inc(self.sum_used, 1)

        class Mix:

            def __init__(self, weight, end, scaled=None, y_high=None, y_low=None):
                self.weight, self.end, self.scaled, self.high, self.low = weight, end, scaled, y_high, y_low
                self.sync = self.store if end == "store" else None

            def __call__(self, ctx, tag, total, mixed, sum_ok, sum_used):
                self.total, self.mixed, self.sum_ok, self.sum_used = total, mixed, sum_ok, sum_used
                self.node = sb(f"node{tag}", [P, 2, BC], ctx=ctx)
                self.feat = sb(f"feat{tag}", [P, 2, BC], ctx=ctx)
                self.last = sb(f"last{tag}", [P, 2, B, C], ctx=ctx)
                (self.node_ok, self.feat_ps, self.feat_ok, self.mix_ps, self.mix_used, self.last_ok, self.part,
                 self.stored) = sems(ctx, *(f"{n}{tag}" for n in (
                     "node_ok", "feat_ps", "feat_ok", "mix_ps", "mix_used", "last_ok", "part", "stored")))
                return self

            def tensor(self, pe, i, u):
                t = 2 * i + u
                if self.scaled is None:
                    pe.wait_ge(self.sum_used, t + 2)
                else:
                    pe.wait_ge(self.node_ok, t + 1)
                for k in range(4):
                    ks = slice(k * P, (k + 1) * P)
                    ins = nc.tensor.transpose(self.mixed[0][:, ks], self.node[:, u, ks], ident[:])
                ins.then_inc(self.feat_ps, 1)
                pe.wait_ge(self.feat_ok, t + 1)
                pe.wait_ge(self.mix_used, t)
                for k in range(4):
                    ks = slice(k * P, (k + 1) * P)
                    ins = nc.tensor.matmul(self.mixed[1][:, ks], self.feat[:, u, ks], self.weight, start=(k == 0),
                                           stop=(k == 3), skip_group_check=True)
                ins.then_inc(self.mix_ps, 1)

            def scalar(self, a, i, u):
                t = 2 * i + u
                if self.scaled is None:
                    a.wait_ge(self.sum_ok, t + 1)
                    nc.scalar.activation(self.node[:, u], self.total[u][:], ACT.Copy).then_inc(self.sum_used, 1)
                a.wait_ge(self.feat_ps, t + 1)
                nc.scalar.activation(self.feat[:, u], self.mixed[0][:], ACT.Copy).then_inc(self.feat_ok, 1)
                if self.end == "split":
                    if u == 0:
                        a.wait_ge(self.part, 2 * i)
                    a.wait_ge(self.mix_ps, t + 1)
                    nc.scalar.activation(self.last[:, u].rearrange("p b c -> p (b c)"), self.mixed[1][:],
                                         ACT.Relu).then_inc(self.mix_used, 1)
                    wait_apart(a, self.mix_used, t + 1)
                    nc.scalar.activation(row(self.high, t), self.last[:, u].rearrange("p b c -> p (b c)"),
                                         ACT.Copy).then_inc(self.last_ok, 1)

            def vector(self, v, i, u):
                t = 2 * i + u
                last = self.last[:, u].rearrange("p b c -> p (b c)")
                if self.scaled is not None:
                    v.wait_ge(self.sum_ok, t + 1)
                    nc.vector.tensor_tensor(self.feat_in(u), self.total[u][:], row(self.scaled, t), ALU.add)\
                        .then_inc(self.sum_used, 1)
                    v.wait_ge(self.sum_used, t + 2)
                    nc.vector.tensor_scalar(self.node[:, u], self.feat_in(u), dinv[:, bass.ds(t, 1)], None,
                                            ALU.mult).then_inc(self.node_ok, 1)
                if self.end == "split":
                    v.wait_ge(self.last_ok, t + 1)
                    nc.vector.tensor_tensor(row(self.low, t), last, row(self.high, t).bitcast(F32), ALU.subtract)\
                        .then_inc(self.part, 1)
                elif self.end == "residual":
                    v.wait_ge(self.mix_ps, t + 1)
                    nc.vector.tensor_tensor(row(res, t), row(res, t), self.mixed[1][:], ALU.add)\
                        .then_inc(self.mix_used, 1)
                else:
                    if u == 0:
                        v.wait_ge(self.stored, 32 * i)
                    v.wait_ge(self.mix_ps, t + 1)
                    nc.vector.scalar_tensor_tensor(out=last, in0=self.mixed[1][:], scalar=0.0, in1=row(res, t),
                                                   op0=ALU.max, op1=ALU.add).then_inc(self.mix_used, 1)

            def feat_in(self, u):
                return self.last[:, u].rearrange("p b c -> p (b c)")

            def store(self, sp):
                rows = out.rearrange("b (t p) c -> p t b c", p=P)
                with sp.Fori(0, T // 2) as i:
                    for u in range(2):
                        sp.wait_ge(self.mix_used, 2 * i + u + 1)
                        sp.dma_start(rows[:, 2 * i + u], self.last[:, u]).then_inc(self.stored, 16)
                sp.wait_ge(self.stored, 16 * T)

        def node_weights(y1, y2):
            with ExitStack() as ctx:
                w_a = sb("w_a", [P, D, O], ctx=ctx)
                w_b = sb("w_b", [C + 1, D, O], ctx=ctx)
                node_a = sb("node_a", [P, B, 2, C], ctx=ctx)
                node_b = sb("node_b", [P, B, C + 1], ctx=ctx)
                feat_a = sb("feat_a", [P, B, P], ctx=ctx)
                feat_b = sb("feat_b", [C + 1, B, P], ctx=ctx)
                emb_t = sb("emb_t", [P, D], ctx=ctx)
                acc = sb("acc", [P, B, O], ctx=ctx)
                turned_a = ps("turned_a", [P, B * P], ctx)
                turned_b = ps("turned_b", [P, B * P], ctx)
                prod = [ps(f"prod{k}", [P, 2, 512], ctx) for k in range(2)]
                w_in, staged, emb_ok, turned_ok, feat_ok, prod_ok, prod_used, steps, row_ok = sems(
                    ctx, "nw_in", "nw_staged", "nw_emb", "nw_turned", "nw_feat", "nw_prod", "nw_used", "nw_steps",
                    "nw_row")
                block = ctx.enter_context(nc.Block())
                DH = D // 2
                UNITS = B

                @block.sync
                def _(sp):
                    rows = l0_w.rearrange("d k i o -> (k i) d o")
                    sp.dma_start(w_a[:], rows[0:P]).then_inc(w_in, 16)
                    sp.dma_start(w_b[0:C], rows[P:P + C]).then_inc(w_in, 16)
                    sp.dma_start(w_b[C:C + 1], l0_b.unsqueeze(0)).then_inc(w_in, 16)
                    sp.wait_ge(w_in, 48)

                @block.scalar
                def _(a):
                    nc.scalar.activation(node_b[:, :, C:C + 1], ones[:, 0:B].unsqueeze(2), ACT.Copy)\
                        .then_inc(row_ok, 1)
                    with a.Fori(0, T) as t:
                        nc.scalar.activation(node_a[:, :, 0, :], act[:, t], ACT.Copy)
                        nc.scalar.activation(node_a[:, :, 1, :], y1[:, t], ACT.Copy)
                        nc.scalar.activation(node_b[:, :, 0:C], y2[:, t], ACT.Copy).then_inc(staged, 1)
                        wait_apart(a, prod_used, UNITS * t + 2)
                        nc.scalar.activation(emb_t[:], emb_s[:, t], ACT.Copy).then_inc(emb_ok, 1)
                        for src, dst in ((turned_a, feat_a), (turned_b, feat_b)):
                            for half in range(2):
                                k = (src is turned_b) * 2 + half
                                a.wait_ge(turned_ok, 4 * t + k + 1)
                                n = dst.shape[0]
                                nc.scalar.activation(
                                    dst[:, 4 * half:4 * half + 4].rearrange("p b n -> p (b n)"),
                                    src[0:n, half * 512:(half + 1) * 512], ACT.Copy).then_inc(feat_ok, 1)

                @block.tensor
                def _(pe):
                    pe.wait_ge(w_in, 48)
                    with pe.Fori(0, T) as t:
                        pe.wait_ge(staged, t + 1)
                        for b in range(B):
                            ins = nc.tensor.transpose(turned_a[:, b * P:(b + 1) * P],
                                                      node_a[:, b].rearrange("p k c -> p (k c)"), ident[:])
                            if b % 4 == 3:
                                ins.then_inc(turned_ok, 1)
                        for b in range(B):
                            ins = nc.tensor.transpose(turned_b[0:C + 1, b * P:(b + 1) * P], node_b[:, b], ident[:])
                            if b % 4 == 3:
                                ins.then_inc(turned_ok, 1)
                        pe.wait_ge(feat_ok, 4 * t + 4)
                        for pair in range(4):
                            for half in range(2):
                                unit = 2 * pair + half
                                dh = slice(half * DH, (half + 1) * DH)
                                pe.wait_ge(prod_used, UNITS * t + unit + 1)
                                for k in range(2):
                                    b = 2 * pair + k
                                    nc.tensor.matmul(prod[half][:, k], feat_a[:, b],
                                                     w_a[:, dh].rearrange("p d o -> p (d o)"),
                                                     start=True, stop=False)
                                    ins = nc.tensor.matmul(prod[half][:, k], feat_b[:, b],
                                                           w_b[:, dh].rearrange("p d o -> p (d o)"),
                                                           start=False, stop=True)
                                ins.then_inc(prod_ok, 1)

                @block.vector
                def _(v):
                    nc.vector.memset(acc[:, 0, 0:1], 0.0).then_inc(prod_used, 1)
                    nc.vector.memset(acc[:, 0, 1:2], 0.0).then_inc(prod_used, 1)
                    v.wait_ge(prod_used, 2)
                    done = Count(steps)
                    with done.over(v, T, B * DH - UNITS) as t:
                        v.wait_ge(emb_ok, t + 1)
                        for pair in range(4):
                            bs = slice(2 * pair, 2 * pair + 2)
                            for half in range(2):
                                unit = 2 * pair + half
                                v.wait_ge(prod_ok, UNITS * t + unit + 1)
                                for d in range(DH):
                                    dd = half * DH + d
                                    if d:
                                        v.wait_ge(steps, done.value)
                                    elif half:
                                        v.wait_ge(prod_used, UNITS * t + unit + 2)
                                    ins = nc.vector.scalar_tensor_tensor(
                                        out=acc[:, bs] if dd < D - 1 else res[:, t, bs],
                                        in0=prod[half][:, :, d * O:(d + 1) * O],
                                        scalar=emb_t[:, dd:dd + 1], in1=acc[:, bs] if dd else res[:, t, bs],
                                        op0=ALU.mult, op1=ALU.add)
                                    if d < DH - 1:
                                        done.add(ins)
                                    else:
                                        ins.then_inc(prod_used, 1)

        class Attention:

            POOL_COLS = N // 4

            def __init__(self, ctx, tag, passes_in_flight):
                F = passes_in_flight
                self.u = sb(f"u{tag}", [P, F, N], F32R, ctx=ctx)
                self.xx_h = sb(f"xx_h{tag}", [P, F, N], F32R, ctx=ctx)
                self.xx_l = sb(f"xx_l{tag}", [P, F, N], F32R, ctx=ctx)
                self.values = sb(f"values{tag}", [P, F, T, C], ctx=ctx)
                self.score = sb(f"score{tag}", [P, 4, N], ctx=ctx)
                self.zero = sb(f"zero{tag}", [P, 2, N], ctx=ctx)
                self.prob_t = sb(f"prob_t{tag}", [P, 2, T, HN], ctx=ctx)
                self.low = sb(f"low{tag}", [P, F, T], ctx=ctx)
                self.sums = sb(f"sums{tag}", [P, F, T], ctx=ctx)
                self.rinv = sb(f"rinv{tag}", [P, F, T], ctx=ctx)
                self.s_ps = [ps(f"s_ps{tag}{k}", [P, N], ctx) for k in range(2)]
                self.turned = [ps(f"turned{tag}{k}", [P, HN], ctx) for k in range(2)]
                self.o_ps = ps(f"o_ps{tag}", [P, HN], ctx)
                self.misc = ps(f"misc{tag}", [P, HN], ctx)
                (self.s_ok, self.s_used, self.zero_ok, self.zero_pool, self.masked_ok, self.exp_ok,
                 self.turned_ok, self.turned_used, self.av_ok, self.av_used, self.rinv_ok, self.misc_ok,
                 self.misc_used, self.start_ok) = sems(ctx, *(f"{n}{tag}" for n in (
                     "s_ok", "s_used", "zero_ok", "zero_pool", "masked_ok", "exp_ok", "turned_ok", "turned_used",
                     "av_ok", "av_used", "rinv_ok", "misc_ok", "misc_used", "start_ok")))

            def begin(self, v, *more):
                credits = (self.s_used, self.s_used, self.turned_used, self.turned_used, self.exp_ok, self.av_ok,
                           self.misc_used, *more)
                for n, sem in enumerate(credits):
                    nc.vector.memset(self.low[:, 0, n % T:n % T + 1], 0.0).then_inc(sem, 1)
                nc.vector.memset(self.sums[:], 1.0).then_inc(self.start_ok, 1)
                nc.vector.memset(self.rinv[:], 1.0).then_inc(self.start_ok, 1)
                nc.vector.memset(self.prob_t[:, 1], 0.0).then_inc(self.start_ok, 1)
                nc.vector.memset(self.o_ps[:], 0.0).then_inc(self.start_ok, 1)
                nc.vector.memset(self.values[:], 0.0).then_inc(self.start_ok, 1)
                v.wait_ge(self.start_ok, 5)

            def scores(self, pe, slot, xx, j, g):
                pe.wait_ge(self.s_used, g + 1)
                rows = self.u[:, slot, j * P:(j + 1) * P]
                for half in range(2):
                    hs = slice(half * HN, (half + 1) * HN)
                    nc.tensor.matmul(self.s_ps[j % 2][:, hs], rows, self.xx_h[:, xx, hs], start=True, stop=False)
                    ins = nc.tensor.matmul(self.s_ps[j % 2][:, hs], rows, self.xx_l[:, xx, hs], start=False,
                                           stop=True)
                ins.then_inc(self.s_ok, 1)

            def turn(self, pe, j, g):
                pe.wait_ge(self.exp_ok, g + 2)
                for k in range(2):
                    pe.wait_ge(self.turned_used, 2 * g + k + 1)
                    for m in range(4):
                        c = (4 * k + m) * P
                        ins = nc.tensor.transpose(self.turned[k][:, m * P:(m + 1) * P],
                                                  self.score[:, j % 4, c:c + P], ident[:])
                    ins.then_inc(self.turned_ok, 1)

            def mix_values(self, pe, slot, half, quarter, n, g_last):
                if quarter == 0:
                    pe.wait_ge(self.turned_used, 2 * g_last + 4)
                    pe.wait_ge(self.av_used, n + 1)
                for m in (2 * quarter, 2 * quarter + 1):
                    ins = nc.tensor.matmul(self.o_ps[(m % 2) * C:(m % 2 + 1) * C, :], self.values[:, slot, m, :],
                                           self.prob_t[:, half, m, :], start=(m < 2), stop=(m >= T - 2),
                                           skip_group_check=True)
                if quarter == 3:
                    ins.then_inc(self.av_ok, 1)

            def multiply(self, v, j, g):
                v.wait_ge(self.s_ok, g + 1)
                nc.vector.tensor_tensor(self.score[:, j % 4, :], self.s_ps[j % 2][:], adjs[:, j, :], ALU.mult)\
                    .then_inc(self.s_used, 1)

            def find_zeros(self, v, j, g):
                v.wait_ge(self.s_used, g + 3)
                cols = slice(self.POOL_COLS, N)
                nc.vector.tensor_scalar(self.zero[:, j % 2, cols], self.score[:, j % 4, cols], 0.0, -NEG_INF,
                                        ALU.is_equal, ALU.mult).then_inc(self.zero_ok, 1)

            def find_zeros_pool(self, pool, j, g):
                wait_apart(pool, self.s_used, g + 3)
                cols = slice(0, self.POOL_COLS)
                nc.gpsimd.tensor_scalar(self.zero[:, j % 2, cols], self.score[:, j % 4, cols], 0.0, -NEG_INF,
                                        ALU.is_equal, ALU.mult).then_inc(self.zero_pool, 1)

            def mask(self, v, slot, j, g):
                wait_apart(v, self.zero_ok, g + 1)
                wait_apart(v, self.zero_pool, g + 1)
                nc.vector.tensor_tensor_reduce(self.score[:, j % 4, :], self.score[:, j % 4, :],
                                               self.zero[:, j % 2, :], 1.0, 3.0e38, ALU.add, ALU.min,
                                               self.low[:, slot, j:j + 1]).then_inc(self.masked_ok, 1)

            def invert(self, v, slot, half, exps):
                v.wait_ge(self.exp_ok, exps + 1)
                hs = slice(4 * half, 4 * half + 4)
                nc.vector.reciprocal(self.rinv[:, slot, hs], self.sums[:, slot, hs]).then_inc(self.rinv_ok, 1)

            def exponents(self, a, slot, j, g):
                a.wait_ge(self.masked_ok, g + 1)
                nc.scalar.activation(self.score[:, j % 4, :], self.score[:, j % 4, :], ACT.Exp, scale=-1.0,
                                     bias=self.low[:, slot, j:j + 1],
                                     accum_out=self.sums[:, slot, j:j + 1]).then_inc(self.exp_ok, 1)

            def keep_turned(self, a, j, g, sums_done):
                for k in range(2):
                    if j % 4 == 0 and k == 0:
                        a.wait_ge(self.av_ok, sums_done + 1)
                    a.wait_ge(self.turned_ok, 2 * g + k + 1)
                    nc.scalar.activation(
                        self.prob_t[:, j // 4, 4 * k:4 * k + 4, (j % 4) * P:(j % 4 + 1) * P],
                        self.turned[k][:].rearrange("p (m n) -> p m n", m=4), ACT.Copy)\
                        .then_inc(self.turned_used, 1)

        def heads(proj):
            with ExitStack() as ctx:
                att = Attention(ctx, "h", 2)
                batch_x = sb("batch_x", [P, T, C], ctx=ctx)
                m_now = sb("m_now", [P, P], F32R, ctx=ctx)
                w_now = sb("w_now", [P, HID + 1 + O], ctx=ctx)
                cat = sb("cat", [P, N], ctx=ctx)
                o_raw = sb("o_raw", [P, HN], ctx=ctx)
                o_norm = sb("o_norm", [P, HN], ctx=ctx)
                diag = sb("diag", [P, 4, P], ctx=ctx)
                biased = sb("biased", [P, HN], ctx=ctx)
                part = sb("part", [P, HN], ctx=ctx)
                batch_ok, values_ok, m_ok, w_ok, xx_high, u_high, diag_ok, cat_ok, proj_ok, zeroed = sems(
                    ctx, "batch_ok", "values_ok", "m_ok", "w_ok", "xx_high", "u_high", "diag_ok", "cat_ok",
                    "proj_ok", "zeroed_h")
                block = ctx.enter_context(nc.Block())
                misc, misc_ok, misc_used = att.misc, att.misc_ok, att.misc_used
                PASSES = B * H

                USES = 7
                SPREAD, CAT = (0, 4), (1, 5)
                U, PROJ = (2, 3), 6
                PER_BATCH = 2 + USES * H

                def base(b, i, s):
                    return 4 + PER_BATCH * b + 2 + 2 * USES * i + USES * s

                def xx_use(b):
                    return 4 + PER_BATCH * b

                def halves(k):
                    return slice(k * HN, (k + 1) * HN)

                def turn_x(pe, use, count):
                    pe.wait_ge(batch_ok, count)
                    for k in range(2):
                        pe.wait_ge(misc_used, use + k + 1)
                        for m in range(4):
                            for side in range(2):
                                ins = nc.tensor.matmul(misc[side * C:(side + 1) * C, m * P:(m + 1) * P],
                                                       batch_x[:, 4 * k + m, :], ident[:], start=True, stop=True,
                                                       skip_group_check=True)
                        ins.then_inc(misc_ok, 1)

                def make_u(pe, use, k, xx, count):
                    pe.wait_ge(m_ok, count)
                    pe.wait_ge(misc_used, use + 1)
                    nc.tensor.matmul(misc[:], m_now[:], att.xx_h[:, xx, halves(k)], start=True, stop=False)
                    nc.tensor.matmul(misc[:], m_now[:], att.xx_l[:, xx, halves(k)], start=False, stop=True)\
                        .then_inc(misc_ok, 1)

                def spread(pe, p, at, half):
                    pe.wait_ge(diag_ok, 2 * p + half + 1)
                    pe.wait_ge(misc_used, at + SPREAD[half] + 1)
                    nc.tensor.matmul(misc[:], ones[:], diag[:].rearrange("p j n -> p (j n)"), start=True, stop=True)\
                        .then_inc(misc_ok, 1)

                def head_out(pe, p, at, half):
                    pe.wait_ge(w_ok, p + 1)
                    pe.wait_ge(misc_used, at + CAT[half] + 1)
                    nc.tensor.matmul(misc[:], w_now[:, 0:HID], o_norm[:], start=True, stop=True).then_inc(misc_ok, 1)

                def project(pe, p, at, w):
                    pe.wait_ge(cat_ok, 2 * p + 2)
                    pe.wait_ge(misc_used, at + PROJ + 1)
                    for k in range(2):
                        ins = nc.tensor.matmul(misc[k * C:(k + 1) * C, :], w, cat[:, halves(k)], start=True,
                                               stop=True, skip_group_check=True)
                    ins.then_inc(misc_ok, 1)

                @block.tensor
                def _(pe):
                    turn_x(pe, 0, 1)
                    for k in range(2):
                        make_u(pe, 2 + k, k, 0, 1)
                    pe.wait_ge(misc_used, 5)
                    for j in range(3):
                        att.scores(pe, 0, 0, j, j)
                    with pe.Fori(0, B) as b:
                        turn_x(pe, xx_use(b), b + 2)
                        with pe.Fori(0, H // 2) as i:
                            for s in range(2):
                                p = H * b + 2 * i + s
                                at = base(b, i, s)
                                xx = b % 2
                                xx_next = xx if s == 0 else ((4 * b + i + 1) // 4) % 2
                                for j in range(T):
                                    g = T * p + j
                                    att.turn(pe, j, g)
                                    if j < 5:
                                        att.scores(pe, s, xx, j + 3, g + 3)
                                    else:
                                        att.scores(pe, 1 - s, xx_next, j - 5, g + 3)
                                    if j < 4:
                                        att.mix_values(pe, 1 - s, 1, j, 2 * p, T * p - 1)
                                    else:
                                        if j == 4:
                                            pe.wait_ge(values_ok, p + 1)
                                        att.mix_values(pe, s, 0, j - 4, 2 * p + 1, T * p + 3)
                                    if j in SPREAD:
                                        spread(pe, p, at, j // 4)
                                    elif j in CAT:
                                        head_out(pe, p, at, j // 4)
                                    elif j in U:
                                        make_u(pe, at + j, j - 2, xx_next, p + 2)
                                    elif j == 7:
                                        project(pe, p, at, w_now[:, HID + 1:])
                    p, at = PASSES, xx_use(B)
                    for quarter in range(4):
                        att.mix_values(pe, 1, 1, quarter, 2 * p, T * p - 1)
                    for half in range(2):
                        spread(pe, p, at + 2 * half - SPREAD[half], half)
                        head_out(pe, p, at + 1 + 2 * half - CAT[half], half)
                    project(pe, p, at + 4 - PROJ, w_now[:, HID + 1:])

                def u_part(a, use, slot, k):
                    a.wait_ge(misc_ok, use + 1)
                    nc.scalar.activation(att.u[:, slot, halves(k)], misc[:], ACT.Copy, scale=-1.0).then_inc(u_high, 1)

                def keep_sum(a, n):
                    a.wait_ge(att.av_ok, n + 2)
                    nc.scalar.activation(o_raw[:], att.o_ps[:], ACT.Copy).then_inc(att.av_used, 1)

                def add_bias(a, p, use, half):
                    if half:
                        a.wait_ge(cat_ok, 2 * p + 1)
                    a.wait_ge(misc_ok, use + 1)
                    nc.scalar.activation(biased[:], misc[:], ACT.Identity, bias=w_now[:, HID:HID + 1])\
                        .then_inc(misc_used, 1)

                def keep_part(a, p, use):
                    a.wait_ge(proj_ok, p + 1)
                    a.wait_ge(misc_ok, use + 1)
                    nc.scalar.activation(part[:], misc[:], ACT.Copy).then_inc(misc_used, 1)

                @block.scalar
                def _(a):
                    a.wait_ge(att.start_ok, 5)
                    for k in range(2):
                        a.wait_ge(misc_ok, k + 1)
                        nc.scalar.activation(att.xx_h[:, 0, halves(k)], misc[:], ACT.Copy).then_inc(xx_high, 1)
                    for k in range(2):
                        u_part(a, 2 + k, 0, k)
                    att.exponents(a, 0, 0, 0)
                    keep_sum(a, -1)
                    with a.Fori(0, B) as b:
                        for k in range(2):
                            wait_apart(a, misc_ok, xx_use(b) + k + 1)
                            nc.scalar.activation(att.xx_h[:, (b + 1) % 2, halves(k)], misc[:], ACT.Copy)\
                                .then_inc(xx_high, 1)
                        with a.Fori(0, H // 2) as i:
                            for s in range(2):
                                p = H * b + 2 * i + s
                                at = base(b, i, s)
                                for j in range(T):
                                    g = T * p + j
                                    if j in (3, 4):
                                        u_part(a, at + U[j - 3], 1 - s, j - 3)
                                    if j == 4:
                                        a.wait_ge(misc_used, at + SPREAD[0] + 2)
                                        keep_sum(a, 2 * p)
                                    att.exponents(a, s if j < T - 1 else 1 - s, (j + 1) % T, g + 1)
                                    if j == 2:
                                        add_bias(a, p, at + CAT[0], 0)
                                    if j == 6:
                                        add_bias(a, p, at + CAT[1], 1)
                                    att.keep_turned(a, j, g, 2 * p + j // 4)
                                a.wait_ge(misc_used, at + SPREAD[1] + 2)
                                keep_sum(a, 2 * p + 1)
                                keep_part(a, p, at + PROJ)
                    p, at = PASSES, xx_use(B)
                    for half in range(2):
                        if half:
                            a.wait_ge(misc_used, at + 2)
                            keep_sum(a, 2 * p)
                        add_bias(a, p, at + 1 + 2 * half, half)
                    keep_part(a, p, at + 4)

                def make_diag(slot, half):
                    nc.gpsimd.tensor_tensor(
                        diag[:], ident[:].unsqueeze(1).to_broadcast([P, 4, P]),
                        att.rinv[:, slot, 4 * half:4 * half + 4].unsqueeze(2).to_broadcast([P, 4, P]),
                        ALU.mult).then_inc(diag_ok, 1)

                @block.gpsimd
                def _(pool):
                    pool.wait_ge(att.start_ok, 5)
                    nc.gpsimd.tensor_copy(batch_x[:], act[:, :, 0, :]).then_inc(batch_ok, 1)
                    nc.gpsimd.tensor_copy(m_now[:], m_split[:, 0, :]).then_inc(m_ok, 1)
                    pool.wait_ge(misc_ok, 2)
                    nc.gpsimd.tensor_copy(batch_x[:], act[:, :, 1, :]).then_inc(batch_ok, 1)
                    pool.wait_ge(misc_ok, 4)
                    nc.gpsimd.tensor_copy(m_now[:], m_split[:, 1, :]).then_inc(m_ok, 1)
                    for j in range(2):
                        att.find_zeros_pool(pool, j, j)
                    nc.gpsimd.memset(part[:], 0.0)
                    nc.gpsimd.memset(proj[:], 0.0).then_inc(zeroed, 1)
                    make_diag(0, 0)
                    pool.wait_ge(zeroed, 1)
                    with pool.Fori(0, B) as b:
                        wait_apart(pool, misc_ok, xx_use(b) + 2)
                        nc.gpsimd.tensor_copy(batch_x[:], act[:, :, (b + 2) % B, :]).then_inc(batch_ok, 1)
                        with pool.Fori(0, H // 2) as i:
                            for s in range(2):
                                p = H * b + 2 * i + s
                                at = base(b, i, s)
                                for j in range(2, T + 2):
                                    att.find_zeros_pool(pool, j % T, T * p + j)
                                    if j == 2:
                                        wait_apart(pool, misc_used, at + 1)
                                        nc.gpsimd.tensor_copy(w_now[:], w_heads[:, (2 * i + s + H - 1) % H, :])\
                                            .then_inc(w_ok, 1)
                                        wait_apart(pool, att.av_ok, 2 * p + 1)
                                        nc.gpsimd.tensor_copy(att.values[:, s], act[:, :, b, :]).then_inc(values_ok, 1)
                                    if j == 3:
                                        slot = (H * b + 2 * i + s + H - 2) // H
                                        nc.gpsimd.tensor_tensor(proj[:, slot, :], proj[:, slot, :], part[:], ALU.add)\
                                            .then_inc(proj_ok, 1)
                                    if j == 4:
                                        wait_apart(pool, misc_ok, at + SPREAD[0] + 1)
                                        wait_apart(pool, att.rinv_ok, 2 * p + 1)
                                        make_diag(1 - s, 1)
                                    if j == 7:
                                        wait_apart(pool, misc_ok, at + U[1] + 1)
                                        nc.gpsimd.tensor_copy(m_now[:], m_split[:, (2 * i + s + 2) % H, :])\
                                            .then_inc(m_ok, 1)
                                    if j == 8:
                                        wait_apart(pool, misc_ok, at + SPREAD[1] + 1)
                                        wait_apart(pool, att.rinv_ok, 2 * p + 2)
                                        make_diag(s, 0)
                    p, at = PASSES, xx_use(B)
                    pool.wait_ge(misc_used, at + 1)
                    nc.gpsimd.tensor_copy(w_now[:], w_heads[:, H - 1, :]).then_inc(w_ok, 1)
                    nc.gpsimd.tensor_tensor(proj[:, B, :], proj[:, B, :], part[:], ALU.add).then_inc(proj_ok, 1)
                    pool.wait_ge(misc_ok, at + 1)
                    pool.wait_ge(att.rinv_ok, 2 * p + 1)
                    make_diag(1, 1)
                    pool.wait_ge(misc_used, at + 6)
                    pool.wait_ge(proj_ok, p + 1)
                    nc.gpsimd.tensor_tensor(proj[:, B, :], proj[:, B, :], part[:], ALU.add).then_inc(proj_ok, 1)

                def u_low(v, count, slot, k):
                    v.wait_ge(u_high, count)
                    nc.vector.scalar_tensor_tensor(out=att.u[C:P, slot, halves(k)], in0=misc[C:P, :], scalar=-1.0,
                                                   in1=att.u[C:P, slot, halves(k)].bitcast(F32), op0=ALU.mult,
                                                   op1=ALU.subtract).then_inc(misc_used, 1)

                def normalise(v, p, use, half):
                    v.wait_ge(att.av_used, 2 * p + half + 1)
                    v.wait_ge(misc_ok, use + 1)
                    nc.vector.tensor_tensor(o_norm[:], o_raw[:], misc[:], ALU.mult).then_inc(misc_used, 1)

                def leaky(v, use, half):
                    v.wait_ge(misc_used, use + 2)
                    nc.vector.scalar_tensor_tensor(out=cat[:, halves(half)], in0=biased[:], scalar=SLOPE,
                                                   in1=biased[:], op0=ALU.mult, op1=ALU.max).then_inc(cat_ok, 1)

                @block.vector
                def _(v):
                    att.begin(v)
                    for k in range(2):
                        v.wait_ge(xx_high, k + 1)
                        nc.vector.tensor_tensor(att.xx_l[:, 0, halves(k)], misc[:],
                                                att.xx_h[:, 0, halves(k)].bitcast(F32), ALU.subtract)\
                            .then_inc(misc_used, 1)
                    for k in range(2):
                        u_low(v, k + 1, 0, k)
                    for j in range(2):
                        att.multiply(v, j, j)
                        att.find_zeros(v, j, j)
                    att.mask(v, 0, 0, 0)
                    with v.Fori(0, B) as b:
                        for k in range(2):
                            v.wait_ge(xx_high, 2 * b + k + 3)
                            nc.vector.tensor_tensor(att.xx_l[:, (b + 1) % 2, halves(k)], misc[:],
                                                    att.xx_h[:, (b + 1) % 2, halves(k)].bitcast(F32), ALU.subtract)\
                                .then_inc(misc_used, 1)
                        with v.Fori(0, H // 2) as i:
                            for s in range(2):
                                p = H * b + 2 * i + s
                                at = base(b, i, s)
                                for j in range(2, T + 2):
                                    g = T * p + j
                                    if j == 4:
                                        normalise(v, p, at + SPREAD[0], 0)
                                    if j in (6, 7):
                                        u_low(v, 2 * p + j - 3, 1 - s, j - 6)
                                    if j == 8:
                                        normalise(v, p, at + SPREAD[1], 1)
                                    att.multiply(v, j % T, g)
                                    att.find_zeros(v, j % T, g)
                                    att.mask(v, s if j <= T else 1 - s, (j - 1) % T, g - 1)
                                    if j == 2:
                                        att.invert(v, 1 - s, 1, T * p)
                                    if j == 5:
                                        att.invert(v, s, 0, T * p + 4)
                                    if j == 6:
                                        leaky(v, at + CAT[0], 0)
                                leaky(v, at + CAT[1], 1)
                    p, at = PASSES, xx_use(B)
                    att.invert(v, 1, 1, T * p)
                    for half in range(2):
                        normalise(v, p, at + 2 * half, half)
                        leaky(v, at + 1 + 2 * half, half)

        def output_attention(proj):
            with ExitStack() as ctx:
                att = Attention(ctx, "o", 1)
                g_now = sb("g_now", [P, HN], ctx=ctx)
                o_sb = sb("o_sb", [P, HN], ctx=ctx)
                y = sb("y", [P, 2, 4, C], ctx=ctx)
                y_leaky = sb("y_leaky", [P, 2, 4, C], ctx=ctx)
                g_ok, xx_high, u_ok, o_copied, y_steps, res_ok = sems(
                    ctx, "g_ok", "xx_high_o", "u_ok", "o_copied", "y_steps", "res_ok")
                block = ctx.enter_context(nc.Block())
                misc, misc_ok, misc_used = att.misc, att.misc_ok, att.misc_used
                PER_PASS = 5

                def halves(k):
                    return slice(k * HN, (k + 1) * HN)

                @block.gpsimd
                def _(pool):
                    pool.wait_ge(att.start_ok, 5)
                    nc.gpsimd.tensor_copy(g_now[:], proj[:, 1, :]).then_inc(g_ok, 1)
                    with pool.Fori(0, B) as p:
                        for j in range(T):
                            att.find_zeros_pool(pool, j, T * p + j)
                            if j == 3:
                                nc.gpsimd.tensor_copy(g_now[:], proj[:, (p + 1) % B + 1, :]).then_inc(g_ok, 1)

                @block.tensor
                def _(pe):
                    with pe.Fori(0, B) as p:
                        at = PER_PASS * p
                        pe.wait_ge(g_ok, p + 1)
                        for k in range(2):
                            pe.wait_ge(misc_used, at + k + 1)
                            nc.tensor.matmul(misc[:], fold[k * C:(k + 1) * C, :], g_now[k * C:(k + 1) * C, :],
                                             start=True, stop=True).then_inc(misc_ok, 1)
                        pe.wait_ge(misc_used, at + 3)
                        for m in range(4):
                            ins = nc.tensor.transpose(misc[:, m * P:(m + 1) * P], g_now[:, m * P:(m + 1) * P],
                                                      ident[:])
                        ins.then_inc(misc_ok, 1)
                        pe.wait_ge(u_ok, 2 * p + 2)
                        for j in range(2):
                            att.scores(pe, 0, 0, j, T * p + j)
                        for j in range(T):
                            g = T * p + j
                            att.turn(pe, j, g)
                            if j + 2 < T:
                                att.scores(pe, 0, 0, j + 2, g + 2)
                            if j % 4 == 3:
                                half = j // 4
                                pe.wait_ge(misc_used, at + 4)
                                for quarter in range(4):
                                    att.mix_values(pe, 0, half, quarter, 2 * p + half, g)
                                pe.wait_ge(misc_used, at + 4 + half)
                                pe.wait_ge(att.av_used, 2 * p + half + 2)
                                for m in range(4):
                                    ins = nc.tensor.matmul(misc[:, m * C:(m + 1) * C], o_sb[:, m * P:(m + 1) * P],
                                                           fold[:, 0:C], start=True, stop=True,
                                                           skip_group_check=True)
                                ins.then_inc(misc_ok, 1)

                def copy_out(a, p, half):
                    a.wait_ge(att.av_ok, 2 * p + half + 2)
                    nc.scalar.activation(o_sb[:], att.o_ps[:], ACT.Copy).then_inc(att.av_used, 1)

                @block.scalar
                def _(a):
                    a.wait_ge(att.start_ok, 5)
                    with a.Fori(0, B) as p:
                        at = PER_PASS * p
                        for k in range(2):
                            a.wait_ge(misc_ok, at + k + 1)
                            nc.scalar.activation(att.xx_h[:, 0, halves(k)], misc[:], ACT.Copy).then_inc(xx_high, 1)
                        a.wait_ge(misc_ok, at + 3)
                        nc.scalar.activation(att.values[:, 0].rearrange("p (a m) c -> p m a c", a=2),
                                             misc[:].rearrange("p (m a c) -> p m a c", m=4, a=2),
                                             ACT.Copy).then_inc(misc_used, 1)
                        for j in range(T):
                            g = T * p + j
                            att.exponents(a, 0, j, g)
                            if j:
                                att.keep_turned(a, j - 1, g - 1, 2 * p + (j - 1) // 4)
                            if j == 4:
                                copy_out(a, p, 0)
                        att.keep_turned(a, T - 1, T * p + T - 1, 2 * p + 1)
                        copy_out(a, p, 1)

                @block.vector
                def _(v):
                    att.begin(v, att.av_used)
                    steps = Count(y_steps)
                    with steps.over(v, B, 10) as p:
                        at = PER_PASS * p

                        def finish(half):
                            att.invert(v, 0, half, T * p + 4 * half + 4)
                            v.wait_ge(misc_ok, at + 4 + half)
                            v.wait_ge(att.rinv_ok, 2 * p + half + 1)
                            for m in range(4):
                                ins = nc.vector.scalar_tensor_tensor(
                                    out=y[:, half, m], in0=misc[:, m * C:(m + 1) * C],
                                    scalar=att.rinv[:, 0, 4 * half + m:4 * half + m + 1], in1=b_proj[:],
                                    op0=ALU.mult, op1=ALU.add)
                                if m < 3:
                                    steps.add(ins)
                                else:
                                    ins.then_inc(misc_used, 1)
                            v.wait_ge(misc_used, at + 5 + half)
                            steps.add(nc.vector.scalar_tensor_tensor(
                                out=y_leaky[:, half], in0=y[:, half], scalar=SLOPE, in1=y[:, half],
                                op0=ALU.mult, op1=ALU.max))
                            v.wait_ge(y_steps, steps.value)
                            ts = slice(4 * half, 4 * half + 4)
                            steps.add(nc.vector.tensor_tensor(res[:, ts, p], res[:, ts, p], y_leaky[:, half],
                                                              ALU.add))

                        for k in range(2):
                            v.wait_ge(xx_high, 2 * p + k + 1)
                            nc.vector.tensor_tensor(att.xx_l[:, 0, halves(k)], misc[:],
                                                    att.xx_h[:, 0, halves(k)].bitcast(F32), ALU.subtract)\
                                .then_inc(misc_used, 1)
                        v.wait_ge(misc_used, at + 3)
                        for part, rows in ((att.xx_h, slice(0, C)), (att.xx_l, slice(C, P))):
                            nc.vector.tensor_scalar(att.u[rows, 0, :], part[rows, 0, :].bitcast(F32), -1.0, None,
                                                    ALU.mult).then_inc(u_ok, 1)
                        for j in range(T):
                            g = T * p + j
                            att.multiply(v, j, g)
                            att.find_zeros(v, j, g)
                            if j:
                                att.mask(v, 0, j - 1, g - 1)
                            if j == 6:
                                finish(0)
                        att.mask(v, 0, T - 1, T * p + T - 1)
                        finish(1)

        def split_tiles(ctx, *names):
            return [sb(n, [P, T, B, C], F32R, ctx=ctx) for n in names]

        with ExitStack() as ctx:
            high, low = split_tiles(ctx, "high", "low")
            y1 = sb("y1", [P, T, B, C], ctx=ctx)
            with ExitStack() as layer0:
                y_high, y_low = split_tiles(layer0, "y1_high", "y1_low")
                y2 = sb("y2", [P, T, B, C], ctx=layer0)
                layernorm("0", high, low)
                graph_product("0", high, low, KeepSplit(y1, y_high, y_low))
                graph_product("1", y_high, y_low, Chebyshev(y2, act))
                node_weights(y1, y2)
            layernorm("1", high, low, scaled=y1)
            graph_product("2", high, low, Mix(bd1[:], "residual", scaled=y1))
            layernorm("2", None, None)
        with ExitStack() as ctx:
            proj = sb("proj", [P, 1 + B, HN], ctx=ctx)
            heads(proj)
            output_attention(proj)
        with ExitStack() as ctx:
            high, low, y_high, y_low = split_tiles(ctx, "high3", "low3", "y_high3", "y_low3")
            layernorm("3", high, low)
            graph_product("3", high, low, Mix(bd3[:, 0], "split", y_high=y_high, y_low=y_low))
            graph_product("4", y_high, y_low, Mix(bd3[:, 1], "store"))


_INS = ["x", "adj", "L0_gnn_embedding", "L0_gnn_weight", "L0_gnn_bias", "L1_gnn_W", "L2_gnn_Wh", "L2_gnn_bh",
        "L2_gnn_W_out", "L2_gnn_b_out", "L3_gnn_net_params"]


def kernel(**inputs):
    import numpy as _np
    import concourse.bacc as _bacc
    from concourse.bass_utils import run_bass_kernel_spmd as _run

    nc = _bacc.Bacc("TRN2", target_bir_lowering=False, num_devices=1)
    arrays, args = {}, []
    for name in _INS:
        a = _np.ascontiguousarray(inputs[name])
        arrays[f"in_{name}"] = a
        args.append(nc.dram_tensor(f"in_{name}", a.shape, mybir.dt.from_np(a.dtype), kind="ExternalInput").ap())
    out = nc.dram_tensor("out", inputs["x"].shape, F32, kind="ExternalOutput").ap()
    build_kernel(nc, *args, out)
    return _run(nc, [arrays], core_ids=[0]).results[0]["out"]
```

```python
from contextlib import ExitStack, contextmanager

import concourse.bass as bass
from concourse import mybir

F32 = mybir.dt.float32
F32R = mybir.dt.float32r
ALU = mybir.AluOpType
ACT = mybir.ActivationFunctionType
AX = mybir.AxisListType

P = 128
NEG_INF = -1e16
EPS = 1e-5
SLOPE = 0.01


def wait_apart(eng, sem, value):
    eng.wait_ge(sem, value)
    eng.nop(nofuse=True)


class Count:

    def __init__(self, sem):
        self.sem, self.value = sem, 0

    def add(self, instruction):
        instruction.then_inc(self.sem, 1)
        self.value = self.value + 1

    @contextmanager
    def over(self, eng, trips, each):
        start = self.value
        with eng.Fori(0, trips) as i:
            self.value = start + i * each
            yield i
        self.value = start + trips * each


def build_kernel(nc, x, adj, emb, l0_w, l0_b, l1_w, wh, bh, w_out, b_out, l3_w, out):
    B, N, C = x.shape
    D, K, _, O = l0_w.shape
    H, _, HID = wh.shape
    T = N // P
    BC = B * C
    HN = N // 2
    G2 = 2 * C
    assert BC == HN == 512 and G2 == P and HID == P and K == 3

    with ExitStack() as whole:
        def sb(name, shape, dt=F32, ctx=whole):
            return ctx.enter_context(nc.sbuf_tensor(name, shape, dt))

        def ps(name, shape, ctx=whole):
            return ctx.enter_context(nc.psum_tensor(name, shape, F32))

        adjs = sb("adjs", [P, T, N])
        res = sb("res", [P, T, B, C])
        act = sb("act", [P, T, B, C])
        emb_s = sb("emb_s", [P, T, D])
        ident = sb("ident", [P, P])
        fold = sb("fold", [P, P])
        ones = sb("ones", [P, P])
        deg = sb("deg", [P, T])
        std = sb("std", [P, T])
        dinv = sb("dinv", [P, T])
        bd1 = sb("bd1", [P, P])
        bd3 = sb("bd3", [P, 2, P])
        w_heads = sb("w_heads", [P, H, HID + 1 + O])
        m_split = sb("m_split", [P, H, P], F32R)
        b_proj = sb("b_proj", [P, O])
        tiny = sb("tiny", [P, 2])

        def sems(ctx, *names):
            return [ctx.enter_context(nc.semaphore(n)) for n in names]

        def split_halves(ap):
            return ap.rearrange("p (t x) -> p t x", t=2)

        class LayerNorm:

            CHUNKS = 4

            NAMES = ("total_ok", "mean_ok", "centred", "squared", "var_ok", "rooted", "rstd_ok", "act_ok",
                     "high_ok", "low_ok", "scaled_ok", "std_ok", "dinv_ok")

            def __init__(self, ctx, tag, past, past_split, high, low, scaled=None):
                self.past, self.past_split, self.high, self.low, self.scaled = past, past_split, high, low, scaled
                G = T * B // self.CHUNKS
                self.square = sb(f"square{tag}", [P, 2, G, C], ctx=ctx)
                self.stat = sb(f"stat{tag}", [P, self.CHUNKS, 5, G], ctx=ctx)
                (self.total_ok, self.mean_ok, self.centred, self.squared, self.var_ok, self.rooted, self.rstd_ok,
                 self.act_ok, self.high_ok, self.low_ok, self.scaled_ok, self.std_ok, self.dinv_ok) = ln_sems

            def groups(self, tile, k):
                n = T // self.CHUNKS
                return tile[:, n * k:n * k + n].rearrange("p t b c -> p (t b) c")

            def split_low(self, engine, k):
                src = act if self.scaled is None else self.scaled
                engine.tensor_tensor(self.groups(self.low, k), self.groups(src, k),
                                     self.groups(self.high, k).bitcast(F32), ALU.subtract).then_inc(self.low_ok, 1)

            def vector(self, v, res_ready=None):
                G = T * B // self.CHUNKS

                def centre(k):
                    total, mean = self.stat[:, k, 0], self.stat[:, k, 1]
                    if res_ready:
                        res_ready(k)
                    nc.vector.tensor_reduce(total, self.groups(res, k), AX.X, ALU.add).then_inc(self.total_ok, 1)
                    v.wait_ge(self.total_ok, self.past + k + 1)
                    nc.vector.tensor_scalar(mean, total, 1.0 / C, None, ALU.mult).then_inc(self.mean_ok, 1)
                    v.wait_ge(self.mean_ok, self.past + k + 1)
                    nc.vector.tensor_tensor(self.groups(act, k), self.groups(res, k),
                                            mean.unsqueeze(2).to_broadcast([P, G, C]), ALU.subtract)\
                        .then_inc(self.centred, 1)

                def variance(k):
                    v.wait_ge(self.squared, self.past + k + 1)
                    nc.vector.tensor_reduce(self.stat[:, k, 2], self.square[:, k % 2], AX.X, ALU.add)\
                        .then_inc(self.var_ok, 1)

                def scale(k):
                    rstd = self.stat[:, k, 4]
                    v.wait_ge(self.rooted, self.past + k + 1)
                    nc.vector.reciprocal(rstd, self.stat[:, k, 3]).then_inc(self.rstd_ok, 1)
                    v.wait_ge(self.rstd_ok, self.past + k + 1)
                    y = self.groups(act, k)
                    nc.vector.scalar_tensor_tensor(out=y, in0=y, scalar=0.0,
                                                   in1=rstd.unsqueeze(2).to_broadcast([P, G, C]), op0=ALU.max,
                                                   op1=ALU.mult).then_inc(self.act_ok, 1)

                if self.scaled is not None:
                    v.wait_ge(self.std_ok, 1)
                    nc.vector.reciprocal(dinv[:], std[:]).then_inc(self.dinv_ok, 1)
                for k in range(self.CHUNKS + 2):
                    if k < self.CHUNKS:
                        centre(k)
                    if k >= 2:
                        scale(k - 2)
                    if 1 <= k <= self.CHUNKS:
                        variance(k - 1)
                if self.high is not None:
                    v.wait_ge(self.high_ok, self.past_split + self.CHUNKS)
                    self.split_low(nc.vector, self.CHUNKS - 1)

            def scalar(self, a):
                def square(k):
                    a.wait_ge(self.centred, self.past + k + 1)
                    if k >= 2:
                        a.wait_ge(self.var_ok, self.past + k - 1)
                    nc.scalar.activation(self.square[:, k % 2], self.groups(act, k), ACT.Square)\
                        .then_inc(self.squared, 1)

                def root(k):
                    a.wait_ge(self.var_ok, self.past + k + 1)
                    nc.scalar.activation(self.stat[:, k, 3], self.stat[:, k, 2], ACT.Sqrt, scale=1.0 / C,
                                         bias=tiny[:, 0:1]).then_inc(self.rooted, 1)

                def split_high(k):
                    a.wait_ge(self.act_ok, self.past + k + 1)
                    src = act
                    if self.scaled is not None:
                        src, n = self.scaled, T // self.CHUNKS
                        for t in range(n * k, n * k + n):
                            ins = nc.scalar.activation(src[:, t], act[:, t], ACT.Copy, scale=dinv[:, t:t + 1])
                        ins.then_inc(self.scaled_ok, 1)
                        a.wait_ge(self.scaled_ok, k + 1)
                    nc.scalar.activation(self.groups(self.high, k), self.groups(src, k), ACT.Copy)\
                        .then_inc(self.high_ok, 1)

                if self.scaled is not None:
                    nc.scalar.activation(std[:], deg[:], ACT.Sqrt, bias=ones[:, 0:1]).then_inc(self.std_ok, 1)
                    a.wait_ge(self.dinv_ok, 1)
                for k in range(self.CHUNKS + 2):
                    if k < self.CHUNKS:
                        square(k)
                    if 1 <= k <= self.CHUNKS:
                        root(k - 1)
                    if k >= 2 and self.high is not None:
                        split_high(k - 2)

            def gpsimd(self, pool):
                if self.high is not None:
                    for k in range(self.CHUNKS - 1):
                        pool.wait_ge(self.high_ok, self.past_split + k + 1)
                        self.split_low(nc.gpsimd, k)

        ln_sems = sems(whole, *(f"ln_{n}" for n in LayerNorm.NAMES))

        def prepare(high, low):
            with ExitStack() as ctx:
                w1_rows = sb("w1_rows", [C, 2, C], ctx=ctx)
                wh_rows = sb("wh_rows", [C, H, HID], ctx=ctx)
                bh_rows = sb("bh_rows", [H, HID], ctx=ctx)
                wh_t = sb("wh_t", [P, H, 2, C], ctx=ctx)
                m_high = sb("m_high", [P, H, P], F32R, ctx=ctx)
                pa = ps("pa", [P, 512], ctx)
                pb = ps("pb", [P, 512], ctx)
                wh_ps = ps("wh_ps", [P, H * C], ctx)
                m_ps = ps("m_ps", [P, H * P], ctx)
                loaded, adj_in, zeroed, ident_ok, consts, pe_done, act_done, dve_done = sems(
                    ctx, "loaded", "adj_in", "zeroed", "ident_ok", "consts", "prep_pe", "prep_act", "prep_dve")
                x_in = sems(ctx, *(f"x_in{k}" for k in range(LayerNorm.CHUNKS)))
                ln = LayerNorm(ctx, "0", 0, 0, high, low)
                block = ctx.enter_context(nc.Block())
                SMALL = 13
                PER_CHUNK = T // LayerNorm.CHUNKS

                @block.sync
                def _(sp):
                    for t in range(T):
                        sp.dma_start(res[:, t], x.rearrange("b (t p) c -> t p b c", p=P)[t])\
                            .then_inc(x_in[t // PER_CHUNK], 16)
                    sp.dma_start(emb_s[:], emb.rearrange("(t p) d -> p t d", p=P)).then_inc(loaded, 16)
                    for k in range(2):
                        sp.dma_start(w1_rows[:, k, :], l1_w).then_inc(loaded, 16)
                    sp.dma_start(wh_rows[:], wh.rearrange("h c d -> c h d")).then_inc(loaded, 16)
                    sp.dma_start(bh_rows[:], bh).then_inc(loaded, 16)
                    for k in range(2):
                        sp.dma_start(w_heads[k * C:(k + 1) * C, :, 0:HID], wh.rearrange("h c d -> c h d"))\
                            .then_inc(loaded, 16)
                    sp.dma_start(w_heads[:, :, HID + 1:], w_out.rearrange("(h d) o -> d h o", d=P)).then_inc(loaded, 16)
                    sp.dma_start(b_proj[:], b_out.partition_broadcast(P)).then_inc(loaded, 16)
                    sp.wait_ge(zeroed, 4)
                    for layer in range(2):
                        for k in range(2):
                            sp.dma_start(bd3[k * C:(k + 1) * C, layer, k * C:(k + 1) * C],
                                        l3_w.rearrange("(l f g) -> l f g", l=2, f=C)[layer]).then_inc(loaded, 16)
                    for t in range(T):
                        sp.dma_start(adjs[:, t, :], adj[t * P:(t + 1) * P, :]).then_inc(adj_in, 16)
                    sp.wait_ge(adj_in, 16 * T)
                    sp.wait_ge(loaded, 16 * SMALL)
                    for sem in x_in:
                        sp.wait_ge(sem, 16 * PER_CHUNK)

                @block.gpsimd
                def _(pool):
                    for tile in (ident, fold, bd1, bd3):
                        nc.gpsimd.memset(tile[:], 0.0).then_inc(zeroed, 1)
                    nc.gpsimd.memset(ones[:], 1.0).then_inc(consts, 1)
                    nc.gpsimd.memset(tiny[:], EPS).then_inc(consts, 1)
                    pool.wait_ge(zeroed, 4)
                    nc.gpsimd.affine_select(out=ident[:], in_=ident[:], compare_op=ALU.not_equal, fill=1.0, base=0,
                                            pattern=[[-1, P]], channel_multiplier=1).then_inc(ident_ok, 1)
                    for n, base in enumerate((0, C, -C)):
                        if n:
                            pool.wait_ge(consts, 2 + n)
                        nc.gpsimd.affine_select(out=fold[:], in_=fold[:], compare_op=ALU.not_equal, fill=1.0,
                                                base=base, pattern=[[-1, P]], channel_multiplier=1).then_inc(consts, 1)
                    ln.gpsimd(pool)

                @block.scalar
                def _(a):
                    a.wait_ge(consts, 2)
                    ln.scalar(a)
                    a.wait_ge(pe_done, 1)
                    for k in range(2):
                        nc.scalar.activation(bd1[k * C:(k + 1) * C, k * C:(k + 1) * C],
                                             pa[k * C:(k + 1) * C, 0:C], ACT.Copy).then_inc(act_done, 1)
                    a.wait_ge(pe_done, 2)
                    nc.scalar.activation(w_heads[:, :, HID], pb[:, 0:H], ACT.Copy).then_inc(act_done, 1)
                    a.wait_ge(pe_done, 3)
                    for k in range(2):
                        ins = nc.scalar.activation(wh_t[:, :, k, :], wh_ps[:].rearrange("p (h c) -> p h c", h=H),
                                                   ACT.Copy)
                    ins.then_inc(act_done, 1)
                    a.wait_ge(pe_done, 4)
                    nc.scalar.activation(m_high[:].rearrange("p h m -> p (h m)"), m_ps[:], ACT.Copy)\
                        .then_inc(act_done, 1)
                    nc.scalar.activation(m_split[0:C].rearrange("p h m -> p (h m)"), m_ps[0:C], ACT.Copy)\
                        .then_inc(act_done, 1)

                @block.tensor
                def _(pe):
                    pe.wait_ge(loaded, 16 * SMALL)
                    pe.wait_ge(ident_ok, 1)
                    nc.tensor.transpose(pa[:, 0:C], w1_rows[:], ident[0:C, 0:C]).then_inc(pe_done, 1)
                    nc.tensor.transpose(pb[:, 0:H], bh_rows[:], ident[0:H, 0:H]).then_inc(pe_done, 1)
                    for h in range(H):
                        ins = nc.tensor.transpose(wh_ps[:, h * C:(h + 1) * C], wh_rows[:, h, :], ident[0:C, 0:C])
                    ins.then_inc(pe_done, 1)
                    pe.wait_ge(act_done, 4)
                    for h in range(H):
                        pair = wh_t[:, h].rearrange("p a c -> p (a c)")
                        ins = nc.tensor.matmul(m_ps[:, h * P:(h + 1) * P], pair, pair, start=True, stop=True,
                                               skip_group_check=True)
                    ins.then_inc(pe_done, 1)

                @block.vector
                def _(v):
                    ln.vector(v, lambda k: v.wait_ge(x_in[k], 16 * PER_CHUNK))
                    v.wait_ge(act_done, 5)
                    nc.vector.tensor_tensor(m_split[C:P].rearrange("p h m -> p (h m)"), m_ps[C:P],
                                            m_high[C:P].rearrange("p h m -> p (h m)").bitcast(F32),
                                            ALU.subtract).then_inc(dve_done, 1)

        def layernorm(tag, past, past_split, high, low, scaled=None):
            with ExitStack() as ctx:
                ln = LayerNorm(ctx, tag, past, past_split, high, low, scaled)
                block = ctx.enter_context(nc.Block())

                @block.scalar
                def _(a):
                    ln.scalar(a)

                @block.vector
                def _(v):
                    ln.vector(v)

                if high is not None:
                    @block.gpsimd
                    def _(pool):
                        ln.gpsimd(pool)

        def graph_product(tag, v_high, v_low, finish, degrees=False):
            with ExitStack() as ctx:
                rows = sb(f"rows{tag}", [P, 2, N], ctx=ctx)
                cols_h = sb(f"cols_h{tag}", [P, 2, N], F32R, ctx=ctx)
                cols_l = sb(f"cols_l{tag}", [P, 2, N], F32R, ctx=ctx)
                credit = sb(f"credit{tag}", [P, 4], ctx=ctx)
                turned = [ps(f"turned{tag}{k}", [P, HN], ctx) for k in range(4)]
                total = [ps(f"total_ps{tag}{k}", [P, BC], ctx) for k in range(2)]
                mixed = [ps(f"mixed{tag}{k}", [P, BC], ctx) for k in range(2)]
                staged, turned_ok, high_ok, low_ok, sum_ok, sum_used = sems(
                    ctx, f"staged{tag}", f"turned_ok{tag}", f"high_ok{tag}", f"low_ok{tag}", f"sum_ok{tag}",
                    f"sum_used{tag}")
                fin = finish(ctx, tag, total, mixed, sum_ok, sum_used)
                block = ctx.enter_context(nc.Block())

                def steps(eng, step):
                    step(0, 0)
                    with eng.Fori(0, (T - 2) // 2) as i:
                        for u in (1, 2):
                            step(2 * i + u, u % 2)
                    step(T - 1, 1)

                def first(t):
                    return isinstance(t, int) and t == 0

                def final(t):
                    return isinstance(t, int) and t == T - 1

                @block.tensor
                def _(pe):
                    def turn(t, u):
                        pe.wait_ge(staged, t + 1)
                        for m in range(T):
                            ins = nc.tensor.transpose(turned[2 * u + m // 4][:, (m % 4) * P:(m % 4 + 1) * P],
                                                      rows[:, u, m * P:(m + 1) * P], ident[:])
                            if m % 4 == 3:
                                ins.then_inc(turned_ok, 1)

                    def multiply(t, u, half):
                        pe.wait_ge(low_ok, 2 * t + half + 1)
                        for m in range(4 * half, 4 * half + 4):
                            mt = slice(m * P, (m + 1) * P)
                            vh = v_high[:, m].rearrange("p b c -> p (b c)")
                            vl = v_low[:, m].rearrange("p b c -> p (b c)")
                            nc.tensor.matmul(total[u][:], cols_h[:, u, mt], vh, start=(m == 0), stop=False)
                            nc.tensor.matmul(total[u][:], cols_h[:, u, mt], vl, start=False, stop=False)
                            ins = nc.tensor.matmul(total[u][:], cols_l[:, u, mt], vh, start=False, stop=(m == T - 1))
                        if half:
                            ins.then_inc(sum_ok, 1)

                    def step(t, u):
                        if not final(t):
                            if not first(t):
                                pe.wait_ge(low_ok, 2 * t)
                            turn(t + 1, 1 - u)
                        if not first(t):
                            pe.wait_ge(sum_used, t)
                        multiply(t, u, 0)
                        if not first(t):
                            fin.turn(pe, t - 1, 1 - u)
                        multiply(t, u, 1)
                        if not first(t):
                            fin.mix(pe, t - 1, 1 - u)

                    turn(0, 0)
                    steps(pe, step)
                    fin.turn(pe, T - 1, 1)
                    fin.mix(pe, T - 1, 1)

                @block.scalar
                def _(a):
                    def stage(t, u):
                        nc.scalar.activation(rows[:, u, :], adjs[:, t, :], ACT.Copy,
                                             accum_out=deg[:, bass.ds(t, 1)] if degrees else None)\
                            .then_inc(staged, 1)

                    def split_high(t, u):
                        for half in range(2):
                            cs = slice(half * HN, (half + 1) * HN)
                            a.wait_ge(turned_ok, 2 * t + half + 1)
                            nc.scalar.activation(cols_h[:, u, cs], turned[2 * u + half][:], ACT.Copy)\
                                .then_inc(high_ok, 1)
                        stage((t + 2) % T, u)

                    def step(t, u):
                        if not first(t):
                            fin.scalar_early(a, t - 1, 1 - u)
                        if not final(t):
                            split_high(t + 1, 1 - u)
                        if not first(t):
                            fin.scalar_late(a, t - 1, 1 - u)

                    for u in range(2):
                        stage(u, u)
                    split_high(0, 0)
                    steps(a, step)
                    fin.scalar_early(a, T - 1, 1)
                    fin.scalar_late(a, T - 1, 1)

                @block.vector
                def _(v):
                    def split_low(t, u):
                        for half in range(2):
                            cs = slice(half * HN, (half + 1) * HN)
                            v.wait_ge(high_ok, 2 * t + half + 1)
                            nc.vector.tensor_tensor(cols_l[:, u, cs], turned[2 * u + half][:],
                                                    cols_h[:, u, cs].bitcast(F32), ALU.subtract).then_inc(low_ok, 1)

                    def step(t, u):
                        if not first(t):
                            fin.vector_early(v, t - 1, 1 - u)
                        if not final(t):
                            split_low(t + 1, 1 - u)
                        if not first(t):
                            fin.vector_late(v, t - 1, 1 - u)

                    for n, sem in enumerate((sum_used, *fin.credits)):
                        nc.vector.memset(credit[:, n:n + 1], 0.0).then_inc(sem, 1)
                    split_low(0, 0)
                    steps(v, step)
                    fin.vector_early(v, T - 1, 1)
                    fin.vector_late(v, T - 1, 1)

                if fin.sync:
                    @block.sync
                    def _(sp):
                        fin.sync(sp)

        def row(tile, t):
            return tile[:, t].rearrange("p b c -> p (b c)")

        class Finish:
            sync = None
            credits = ()

            def turn(self, pe, t, u):
                pass

            mix = scalar_early = scalar_late = vector_early = vector_late = turn

        class KeepSplit(Finish):

            def __init__(self, y, y_high, y_low):
                self.y, self.high, self.low = y, y_high, y_low

            def __call__(self, ctx, tag, total, mixed, sum_ok, sum_used):
                self.total, self.sum_ok, self.sum_used = total, sum_ok, sum_used
                self.split_ok, = sems(ctx, f"split_ok{tag}")
                return self

            def scalar_early(self, a, t, u):
                wait_apart(a, self.sum_ok, t + 1)
                nc.scalar.activation(row(self.y, t), self.total[u][:], ACT.Copy)
                nc.scalar.activation(row(self.high, t), self.total[u][:], ACT.Copy).then_inc(self.split_ok, 1)

            def vector_late(self, v, t, u):
                v.wait_ge(self.split_ok, t + 1)
                nc.vector.tensor_tensor(row(self.low, t), self.total[u][:], row(self.high, t).bitcast(F32),
                                        ALU.subtract).then_inc(self.sum_used, 1)

        class Chebyshev(Finish):

            def __init__(self, y, x):
                self.y, self.x = y, x

            def __call__(self, ctx, tag, total, mixed, sum_ok, sum_used):
                self.total, self.sum_ok, self.sum_used = total, sum_ok, sum_used
                return self

            def vector_early(self, v, t, u):
                v.wait_ge(self.sum_ok, t + 1)
                nc.vector.scalar_tensor_tensor(out=row(self.y, t), in0=self.total[u][:], scalar=2.0,
                                               in1=row(self.x, t), op0=ALU.mult, op1=ALU.subtract)\
                    .then_inc(self.sum_used, 1)

        class Mix(Finish):

            def __init__(self, weight, end, scaled=None, y_high=None, y_low=None):
                self.weight, self.end, self.scaled, self.high, self.low = weight, end, scaled, y_high, y_low
                self.sync = self.store if end == "store" else None

            def __call__(self, ctx, tag, total, mixed, sum_ok, sum_used):
                self.total, self.mixed, self.sum_ok, self.sum_used = total, mixed, sum_ok, sum_used
                self.node = sb(f"node{tag}", [P, 2, BC], ctx=ctx)
                self.feat = sb(f"feat{tag}", [P, 2, BC], ctx=ctx)
                self.last = sb(f"last{tag}", [P, 2, BC], ctx=ctx)
                (self.node_ok, self.feat_ps, self.feat_ok, self.mix_ps, self.mix_used, self.last_ok, self.part,
                 self.stored) = sems(ctx, *(f"{n}{tag}" for n in (
                     "node_ok", "feat_ps", "feat_ok", "mix_ps", "mix_used", "last_ok", "part", "stored")))
                self.credits = (self.mix_used, self.part, self.part)
                return self

            def turn(self, pe, t, u):
                if self.scaled is None:
                    pe.wait_ge(self.sum_used, t + 2)
                else:
                    pe.wait_ge(self.node_ok, t + 1)
                for k in range(4):
                    ks = slice(k * P, (k + 1) * P)
                    ins = nc.tensor.transpose(self.mixed[0][:, ks], self.node[:, u, ks], ident[:])
                ins.then_inc(self.feat_ps, 1)

            def mix(self, pe, t, u):
                pe.wait_ge(self.feat_ok, t + 1)
                pe.wait_ge(self.mix_used, t + 1)
                for k in range(4):
                    ks = slice(k * P, (k + 1) * P)
                    ins = nc.tensor.matmul(self.mixed[1][:, ks], self.feat[:, u, ks], self.weight, start=(k == 0),
                                           stop=(k == 3), skip_group_check=True)
                ins.then_inc(self.mix_ps, 1)

            def scalar_early(self, a, t, u):
                if self.scaled is None:
                    a.wait_ge(self.sum_ok, t + 1)
                    nc.scalar.activation(self.node[:, u], self.total[u][:], ACT.Copy).then_inc(self.sum_used, 1)

            def scalar_late(self, a, t, u):
                a.wait_ge(self.feat_ps, t + 1)
                nc.scalar.activation(self.feat[:, u], self.mixed[0][:], ACT.Copy).then_inc(self.feat_ok, 1)
                if self.end == "split":
                    a.wait_ge(self.part, t + 1)
                    a.wait_ge(self.mix_ps, t + 1)
                    nc.scalar.activation(self.last[:, u], self.mixed[1][:], ACT.Relu).then_inc(self.mix_used, 1)
                    wait_apart(a, self.mix_used, t + 2)
                    nc.scalar.activation(row(self.high, t), self.last[:, u], ACT.Copy).then_inc(self.last_ok, 1)

            def vector_early(self, v, t, u):
                if self.scaled is not None:
                    v.wait_ge(self.sum_ok, t + 1)
                    nc.vector.tensor_tensor(self.last[:, u], self.total[u][:], row(self.scaled, t), ALU.add)\
                        .then_inc(self.sum_used, 1)
                    v.wait_ge(self.sum_used, t + 2)
                    nc.vector.tensor_scalar(self.node[:, u], self.last[:, u], dinv[:, bass.ds(t, 1)], None,
                                            ALU.mult).then_inc(self.node_ok, 1)

            def vector_late(self, v, t, u):
                if self.end == "split":
                    v.wait_ge(self.last_ok, t + 1)
                    nc.vector.tensor_tensor(row(self.low, t), self.last[:, u], row(self.high, t).bitcast(F32),
                                            ALU.subtract).then_inc(self.part, 1)
                    return
                v.wait_ge(self.mix_ps, t + 1)
                if self.end == "residual":
                    nc.vector.tensor_tensor(row(res, t), row(res, t), self.mixed[1][:], ALU.add)\
                        .then_inc(self.mix_used, 1)
                else:
                    nc.vector.scalar_tensor_tensor(out=row(res, t), in0=self.mixed[1][:], scalar=0.0,
                                                   in1=row(res, t), op0=ALU.max, op1=ALU.add)\
                        .then_inc(self.mix_used, 1)

            def store(self, sp):
                rows = out.rearrange("b (t p) c -> p t b c", p=P)
                with sp.Fori(0, T) as t:
                    sp.wait_ge(self.mix_used, t + 2)
                    sp.dma_start(rows[:, t], res[:, t]).then_inc(self.stored, 16)
                sp.wait_ge(self.stored, 16 * T)

        def node_weights(y1, y2):
            with ExitStack() as ctx:
                w_rows = sb("w_rows", [P, 2, D, O], ctx=ctx)
                w_high = sb("w_high", [P, 2, D, O], F32R, ctx=ctx)
                w_low = sb("w_low", [P, 2, D, O], F32R, ctx=ctx)
                bias_rows = sb("bias_rows", [D, O], ctx=ctx)
                emb_turned = sb("emb_turned", [D, N], ctx=ctx)
                node_a = sb("node_a", [P, B, 2, C], ctx=ctx)
                node_b = sb("node_b", [P, B, 2, C], ctx=ctx)
                feat_h = sb("feat_h", [P, 2, B, P], F32R, ctx=ctx)
                feat_l = sb("feat_l", [P, 2, B, P], F32R, ctx=ctx)
                feat_b = sb("feat_b", [P, 2, B, P], F32R, ctx=ctx)
                emb_t = sb("emb_t", [P, 2, D], ctx=ctx)
                acc = sb("acc", [P, 2, 2, 2, O], ctx=ctx)
                turned_a = ps("turned_a", [P, B * P], ctx)
                turned_b = ps("turned_b", [P, B * P], ctx)
                prod = [ps(f"prod{k}", [P, 2, 512], ctx) for k in range(2)]
                (w_in, w_high_ok, w_low_ok, staged, emb_ok, turned_ok, high_ok, low_ok, prod_ok, prod_used, steps,
                 bias_ps, bias_ok, bias_in, emb_steps) = sems(
                    ctx, "nw_in", "nw_w_high", "nw_w_low", "nw_staged", "nw_emb", "nw_turned", "nw_high", "nw_low",
                    "nw_prod", "nw_used", "nw_steps", "nw_bias_ps", "nw_bias_ok", "nw_bias_in", "nw_emb_steps")
                block = ctx.enter_context(nc.Block())
                DH = D // 2
                UNITS = B

                @block.sync
                def _(sp):
                    rows = l0_w.rearrange("d k i o -> (k i) d o")
                    sp.dma_start(bias_rows[:], l0_b).then_inc(bias_in, 16)
                    sp.dma_start(w_rows[:, 0], rows[0:P]).then_inc(w_in, 16)
                    for k in range(2):
                        sp.dma_start(w_rows[k * C:(k + 1) * C, 1], rows[P:P + C]).then_inc(w_in, 16)
                    sp.wait_ge(bias_in, 16)
                    sp.wait_ge(w_in, 48)

                def bank(tile, half):
                    return tile[:, half * 512:(half + 1) * 512]

                @block.scalar
                def _(a):
                    def stage(t):
                        nc.scalar.activation(node_a[:, :, 0, :], act[:, t], ACT.Copy)
                        nc.scalar.activation(node_a[:, :, 1, :], y1[:, t], ACT.Copy)
                        nc.scalar.activation(node_b[:, :, 0, :], y2[:, t], ACT.Copy)
                        nc.scalar.activation(node_b[:, :, 1, :], y2[:, t], ACT.Copy).then_inc(staged, 1)

                    def stage_emb(t, u):
                        nc.scalar.activation(emb_t[:, u], emb_s[:, t], ACT.Copy).then_inc(emb_ok, 1)

                    def split_high(t, u):
                        for n, (src, dst) in enumerate(((turned_a, feat_h), (turned_b, feat_b))):
                            for half in range(2):
                                a.wait_ge(turned_ok, 4 * t + 2 * n + half + 1)
                                nc.scalar.activation(dst[:, u, 4 * half:4 * half + 4].rearrange("p b n -> p (b n)"),
                                                     bank(src, half), ACT.Copy).then_inc(high_ok, 1)

                    for half in range(2):
                        a.wait_ge(bias_ps, half + 1)
                        nc.scalar.activation(emb_turned[:, half * 512:(half + 1) * 512],
                                             turned_a[0:D, half * 512:(half + 1) * 512], ACT.Copy)\
                            .then_inc(emb_steps, 1)
                    stage(0)
                    stage_emb(0, 0)
                    split_high(0, 0)
                    stage(1)
                    a.wait_ge(w_in, 48)
                    for k in range(2):
                        nc.scalar.activation(w_high[:, k], w_rows[:, k], ACT.Copy).then_inc(w_high_ok, 1)
                    with a.Fori(0, T // 2) as i:
                        for u in range(2):
                            t = 2 * i + u
                            wait_apart(a, prod_used, UNITS * t + 2)
                            stage_emb((t + 1) % T, 1 - u)
                            split_high(t + 1, 1 - u)
                            stage((t + 2) % T)

                @block.tensor
                def _(pe):
                    def turn(node, turned):
                        for b in range(B):
                            ins = nc.tensor.transpose(turned[:, b * P:(b + 1) * P],
                                                      node[:, b].rearrange("p k c -> p (k c)"), ident[:])
                            if b % 4 == 3:
                                ins.then_inc(turned_ok, 1)

                    for t in range(T):
                        ins = nc.tensor.transpose(turned_a[0:D, t * P:(t + 1) * P], emb_s[:, t], ident[:])
                        if t % 4 == 3:
                            ins.then_inc(bias_ps, 1)
                    pe.wait_ge(bias_in, 16)
                    pe.wait_ge(emb_steps, 2)
                    for t in range(T):
                        ins = nc.tensor.matmul(turned_b[:, t * O:(t + 1) * O], emb_turned[:, t * P:(t + 1) * P],
                                               bias_rows[:], start=True, stop=True, skip_group_check=True)
                    ins.then_inc(bias_ps, 1)
                    pe.wait_ge(staged, 1)
                    turn(node_a, turned_a)
                    pe.wait_ge(bias_ok, 1)
                    turn(node_b, turned_b)
                    pe.wait_ge(w_low_ok, 2)
                    with pe.Fori(0, T // 2) as i:
                        for u in range(2):
                            t = 2 * i + u
                            pe.wait_ge(low_ok, 4 * t + 4)
                            for unit in range(UNITS):
                                pair, half = unit // 2, unit % 2
                                dh = slice(half * DH, (half + 1) * DH)
                                wide = [w[:, k, dh].rearrange("p d o -> p (d o)")
                                        for k in range(2) for w in (w_high, w_low)]
                                pe.wait_ge(prod_used, UNITS * t + unit + 1)
                                for k in range(2):
                                    b = 2 * pair + k
                                    out_ps = prod[half][:, k]
                                    nc.tensor.matmul(out_ps, feat_h[:, u, b], wide[0], start=True, stop=False)
                                    nc.tensor.matmul(out_ps, feat_h[:, u, b], wide[1], start=False, stop=False)
                                    nc.tensor.matmul(out_ps, feat_l[:, u, b], wide[0], start=False, stop=False)
                                    nc.tensor.matmul(out_ps, feat_b[:, u, b], wide[2], start=False, stop=False)
                                    ins = nc.tensor.matmul(out_ps, feat_b[0:C, u, b], wide[3][0:C], start=False,
                                                           stop=True)
                                ins.then_inc(prod_ok, 1)
                                if unit == 1:
                                    pe.wait_ge(staged, t + 2)
                                    turn(node_a, turned_a)
                                if unit == 3:
                                    turn(node_b, turned_b)

                @block.vector
                def _(v):
                    def split_low(t, u, which):
                        for half in range(2):
                            bs = slice(4 * half, 4 * half + 4)
                            v.wait_ge(high_ok, 4 * t + 2 * which + half + 1)
                            if which == 0:
                                out_ap, high = feat_l[:, u, bs], feat_h[:, u, bs]
                                src = bank(turned_a, half)
                            else:
                                out_ap = high = feat_b[C:P, u, bs]
                                src = bank(turned_b, half)[C:P]
                            nc.vector.tensor_tensor(out_ap.rearrange("p b n -> p (b n)"), src,
                                                    high.bitcast(F32).rearrange("p b n -> p (b n)"),
                                                    ALU.subtract).then_inc(low_ok, 1)

                    nc.vector.memset(acc[:, 0, 0, 0, 0:1], 0.0).then_inc(prod_used, 1)
                    nc.vector.memset(acc[:, 0, 0, 0, 1:2], 0.0).then_inc(prod_used, 1)
                    v.wait_ge(prod_used, 2)
                    v.wait_ge(bias_ps, 3)
                    nc.vector.tensor_tensor(res[:], res[:], turned_b[:, 0:T * O].rearrange("p (t c) -> p t c", t=T)
                                            .unsqueeze(2).to_broadcast([P, T, B, C]), ALU.add).then_inc(bias_ok, 1)
                    for which in range(2):
                        split_low(0, 0, which)
                    for k in range(2):
                        v.wait_ge(w_high_ok, k + 1)
                        nc.vector.tensor_tensor(w_low[:, k], w_rows[:, k], w_high[:, k].bitcast(F32),
                                                ALU.subtract).then_inc(w_low_ok, 1)
                    v.wait_ge(bias_ok, 1)
                    done = Count(steps)
                    done.add(nc.vector.memset(acc[:, 0, 1, 0, 0:1], 0.0))
                    PER_TILE = 4 * (2 * (DH - 1) + 1)
                    with done.over(v, T // 2, 2 * PER_TILE) as i:
                        for u in range(2):
                            t = 2 * i + u
                            v.wait_ge(emb_ok, t + 1)

                            def add_up(pair):
                                done.add(nc.vector.tensor_tensor(
                                    res[:, t, 2 * pair:2 * pair + 2], acc[:, pair % 2, 0], acc[:, pair % 2, 1],
                                    ALU.add))

                            for pair in range(4):
                                bs = slice(2 * pair, 2 * pair + 2)
                                sums = acc[:, pair % 2]
                                for half in range(2):
                                    unit = 2 * pair + half
                                    v.wait_ge(prod_ok, UNITS * t + unit + 1)
                                    for d in range(DH):
                                        dd = half * DH + d
                                        src, weight = prod[half][:, :, d * O:(d + 1) * O], emb_t[:, u, dd:dd + 1]
                                        if half and d == 1:
                                            v.wait_ge(prod_used, UNITS * t + unit + 2)
                                        elif d == 0:
                                            v.wait_ge(steps, done.value)
                                        elif dd == 2 and pair:
                                            v.wait_ge(steps, done.value - 2)
                                        elif dd > 1:
                                            v.wait_ge(steps, done.value - 1)
                                        if dd == 1:
                                            ins = nc.vector.tensor_scalar(sums[:, 1], src, weight, None, ALU.mult)
                                        else:
                                            ins = nc.vector.scalar_tensor_tensor(
                                                out=sums[:, d % 2], in0=src, scalar=weight,
                                                in1=sums[:, d % 2] if dd else res[:, t, bs],
                                                op0=ALU.mult, op1=ALU.add)
                                        if d < DH - 1:
                                            done.add(ins)
                                        else:
                                            ins.then_inc(prod_used, 1)
                                        if dd == 1 and pair:
                                            v.wait_ge(prod_used, UNITS * t + unit + 2)
                                            add_up(pair - 1)
                                if pair in (1, 2):
                                    split_low(t + 1, 1 - u, pair - 1)
                            v.wait_ge(prod_used, UNITS * t + UNITS + 2)
                            v.wait_ge(steps, done.value)
                            add_up(3)

        class Attention:

            POOL_COLS = 3 * N // 8

            def __init__(self, ctx, tag, passes_in_flight):
                F = passes_in_flight
                self.u = sb(f"u{tag}", [P, F, N], F32R, ctx=ctx)
                self.xx_h = sb(f"xx_h{tag}", [P, F, N], F32R, ctx=ctx)
                self.xx_l = sb(f"xx_l{tag}", [P, F, N], F32R, ctx=ctx)
                self.values = sb(f"values{tag}", [P, F, T, C], ctx=ctx)
                self.score = sb(f"score{tag}", [P, 4, N], ctx=ctx)
                self.zero = sb(f"zero{tag}", [P, 2, N], ctx=ctx)
                self.prob_t = sb(f"prob_t{tag}", [P, 2, T, HN], ctx=ctx)
                self.low = sb(f"low{tag}", [P, F, T], ctx=ctx)
                self.sums = sb(f"sums{tag}", [P, F, T], ctx=ctx)
                self.rinv = sb(f"rinv{tag}", [P, F, T], ctx=ctx)
                self.s_ps = [ps(f"s_ps{tag}{k}", [P, N], ctx) for k in range(2)]
                self.turned = [ps(f"turned{tag}{k}", [P, HN], ctx) for k in range(2)]
                self.o_ps = ps(f"o_ps{tag}", [P, HN], ctx)
                self.misc = ps(f"misc{tag}", [P, HN], ctx)
                (self.s_ok, self.s_used, self.zero_ok, self.zero_pool, self.masked_ok, self.exp_ok,
                 self.turned_ok, self.turned_used, self.av_ok, self.av_used, self.rinv_ok, self.misc_ok,
                 self.misc_used, self.start_ok) = sems(ctx, *(f"{n}{tag}" for n in (
                     "s_ok", "s_used", "zero_ok", "zero_pool", "masked_ok", "exp_ok", "turned_ok", "turned_used",
                     "av_ok", "av_used", "rinv_ok", "misc_ok", "misc_used", "start_ok")))

            def begin(self, v):
                credits = (self.s_used, self.s_used, self.turned_used, self.turned_used, self.exp_ok, self.av_ok,
                           self.misc_used)
                for n, sem in enumerate(credits):
                    nc.vector.memset(self.low[:, 0, n % T:n % T + 1], 0.0).then_inc(sem, 1)
                nc.vector.memset(self.sums[:], 1.0).then_inc(self.start_ok, 1)
                nc.vector.memset(self.rinv[:], 1.0).then_inc(self.start_ok, 1)
                nc.vector.memset(self.o_ps[:], 0.0).then_inc(self.start_ok, 1)

            def begin_gpsimd(self, pool):
                nc.gpsimd.memset(self.values[:, 1], 0.0).then_inc(self.start_ok, 1)
                nc.gpsimd.memset(self.prob_t[:, 1], 0.0).then_inc(self.start_ok, 1)

            def scores(self, pe, slot, xx, j, g):
                pe.wait_ge(self.s_used, g + 1)
                rows = self.u[:, slot, j * P:(j + 1) * P]
                for half in range(2):
                    hs = slice(half * HN, (half + 1) * HN)
                    nc.tensor.matmul(self.s_ps[j % 2][:, hs], rows, self.xx_h[:, xx, hs], start=True, stop=False)
                    ins = nc.tensor.matmul(self.s_ps[j % 2][:, hs], rows, self.xx_l[:, xx, hs], start=False,
                                           stop=True)
                ins.then_inc(self.s_ok, 1)

            def turn(self, pe, j, g):
                pe.wait_ge(self.exp_ok, g + 2)
                for k in range(2):
                    pe.wait_ge(self.turned_used, 2 * g + k + 1)
                    for m in range(4):
                        c = (4 * k + m) * P
                        ins = nc.tensor.transpose(self.turned[k][:, m * P:(m + 1) * P],
                                                  self.score[:, j % 4, c:c + P], ident[:])
                    ins.then_inc(self.turned_ok, 1)

            def mix_values(self, pe, slot, half, quarter, n, g_last):
                if quarter == 0:
                    pe.wait_ge(self.turned_used, 2 * g_last + 4)
                    pe.wait_ge(self.av_used, n + 1)
                for m in (2 * quarter, 2 * quarter + 1):
                    ins = nc.tensor.matmul(self.o_ps[(m % 2) * C:(m % 2 + 1) * C, :], self.values[:, slot, m, :],
                                           self.prob_t[:, half, m, :], start=(m < 2), stop=(m >= T - 2),
                                           skip_group_check=True)
                if quarter == 3:
                    ins.then_inc(self.av_ok, 1)

            def multiply(self, v, j, g):
                v.wait_ge(self.s_ok, g + 1)
                nc.vector.tensor_tensor(self.score[:, j % 4, :], self.s_ps[j % 2][:], adjs[:, j, :], ALU.mult)\
                    .then_inc(self.s_used, 1)

            def find_zeros(self, v, j, g):
                v.wait_ge(self.s_used, g + 3)
                cols = slice(self.POOL_COLS, N)
                nc.vector.tensor_scalar(self.zero[:, j % 2, cols], self.score[:, j % 4, cols], 0.0, -NEG_INF,
                                        ALU.is_equal, ALU.mult).then_inc(self.zero_ok, 1)

            def find_zeros_pool(self, pool, j, g):
                wait_apart(pool, self.s_used, g + 3)
                cols = slice(0, self.POOL_COLS)
                nc.gpsimd.tensor_scalar(self.zero[:, j % 2, cols], self.score[:, j % 4, cols], 0.0, -NEG_INF,
                                        ALU.is_equal, ALU.mult).then_inc(self.zero_pool, 1)

            def mask(self, v, slot, j, g):
                wait_apart(v, self.zero_ok, g + 1)
                wait_apart(v, self.zero_pool, g + 1)
                nc.vector.tensor_tensor_reduce(self.score[:, j % 4, :], self.score[:, j % 4, :],
                                               self.zero[:, j % 2, :], 1.0, 3.0e38, ALU.add, ALU.min,
                                               self.low[:, slot, j:j + 1]).then_inc(self.masked_ok, 1)

            def invert(self, v, slot, half, exps):
                v.wait_ge(self.exp_ok, exps + 1)
                hs = slice(4 * half, 4 * half + 4)
                nc.vector.reciprocal(self.rinv[:, slot, hs], self.sums[:, slot, hs]).then_inc(self.rinv_ok, 1)

            def exponents(self, a, slot, j, g):
                a.wait_ge(self.masked_ok, g + 1)
                nc.scalar.activation(self.score[:, j % 4, :], self.score[:, j % 4, :], ACT.Exp, scale=-1.0,
                                     bias=self.low[:, slot, j:j + 1],
                                     accum_out=self.sums[:, slot, j:j + 1]).then_inc(self.exp_ok, 1)

            def keep_turned(self, a, j, g, sums_done):
                for k in range(2):
                    if j % 4 == 0 and k == 0:
                        a.wait_ge(self.av_ok, sums_done + 1)
                    a.wait_ge(self.turned_ok, 2 * g + k + 1)
                    nc.scalar.activation(
                        self.prob_t[:, j // 4, 4 * k:4 * k + 4, (j % 4) * P:(j % 4 + 1) * P],
                        self.turned[k][:].rearrange("p (m n) -> p m n", m=4), ACT.Copy)\
                        .then_inc(self.turned_used, 1)

        def heads(proj):
            with ExitStack() as ctx:
                att = Attention(ctx, "h", 2)
                batch_x = sb("batch_x", [P, T, 2, C], ctx=ctx)
                m_now = sb("m_now", [P, P], F32R, ctx=ctx)
                w_now = sb("w_now", [P, HID + 1 + O], ctx=ctx)
                cat = sb("cat", [P, N], ctx=ctx)
                o_raw = sb("o_raw", [P, HN], ctx=ctx)
                o_norm = sb("o_norm", [P, HN], ctx=ctx)
                rinv_split = sb("rinv_split", [P, 2, 4], F32R, ctx=ctx)
                diag = sb("diag", [P, 2, 4, P], F32R, ctx=ctx)
                ones_r = sb("ones_r", [P, P], F32R, ctx=ctx)
                biased = sb("biased", [P, HN], ctx=ctx)
                part = sb("part", [P, HN], ctx=ctx)
                (batch_ok, values_ok, m_ok, w_ok, xx_high, u_high, diag_ok, cat_ok, proj_ok, zeroed,
                 diag_steps) = sems(
                    ctx, "batch_ok", "values_ok", "m_ok", "w_ok", "xx_high", "u_high", "diag_ok", "cat_ok",
                    "proj_ok", "zeroed_h", "diag_steps")
                block = ctx.enter_context(nc.Block())
                misc, misc_ok, misc_used = att.misc, att.misc_ok, att.misc_used
                PASSES = B * H

                USES = 7
                SPREAD, CAT = (0, 4), (1, 5)
                U, PROJ = (2, 3), 6
                PER_BATCH = 2 + USES * H

                def base(b, i, s):
                    return 4 + PER_BATCH * b + 2 + 2 * USES * i + USES * s

                def xx_use(b):
                    return 4 + PER_BATCH * b

                def halves(k):
                    return slice(k * HN, (k + 1) * HN)

                def turn_x(pe, use, count):
                    pe.wait_ge(batch_ok, count)
                    for k in range(2):
                        pe.wait_ge(misc_used, use + k + 1)
                        for m in range(4):
                            ins = nc.tensor.transpose(misc[:, m * P:(m + 1) * P],
                                                      batch_x[:, 4 * k + m].rearrange("p k c -> p (k c)"), ident[:])
                        ins.then_inc(misc_ok, 1)

                def make_u(pe, use, k, xx, count):
                    pe.wait_ge(m_ok, count)
                    pe.wait_ge(misc_used, use + 1)
                    nc.tensor.matmul(misc[:], m_now[:], att.xx_h[:, xx, halves(k)], start=True, stop=False)
                    nc.tensor.matmul(misc[:], m_now[:], att.xx_l[:, xx, halves(k)], start=False, stop=True)\
                        .then_inc(misc_ok, 1)

                def spread(pe, p, at, half):
                    pe.wait_ge(diag_ok, 2 * p + half + 1)
                    pe.wait_ge(misc_used, at + SPREAD[half] + 1)
                    for k in range(2):
                        ins = nc.tensor.matmul(misc[:], ones_r[:], diag[:, k].rearrange("p j n -> p (j n)"),
                                               start=(k == 0), stop=(k == 1))
                    ins.then_inc(misc_ok, 1)

                def head_out(pe, p, at, half):
                    pe.wait_ge(w_ok, p + 1)
                    pe.wait_ge(misc_used, at + CAT[half] + 1)
                    nc.tensor.matmul(misc[:], w_now[:, 0:HID], o_norm[:], start=True, stop=True).then_inc(misc_ok, 1)

                def project(pe, p, at, w):
                    pe.wait_ge(cat_ok, 2 * p + 2)
                    pe.wait_ge(misc_used, at + PROJ + 1)
                    for k in range(2):
                        ins = nc.tensor.matmul(misc[k * C:(k + 1) * C, :], w, cat[:, halves(k)], start=True,
                                               stop=True, skip_group_check=True)
                    ins.then_inc(misc_ok, 1)

                @block.tensor
                def _(pe):
                    turn_x(pe, 0, 1)
                    for k in range(2):
                        make_u(pe, 2 + k, k, 0, 1)
                    pe.wait_ge(misc_used, 5)
                    for j in range(3):
                        att.scores(pe, 0, 0, j, j)
                    pe.wait_ge(att.start_ok, 5)
                    with pe.Fori(0, B) as b:
                        turn_x(pe, xx_use(b), b + 2)
                        with pe.Fori(0, H // 2) as i:
                            for s in range(2):
                                p = H * b + 2 * i + s
                                at = base(b, i, s)
                                xx = b % 2
                                xx_next = xx if s == 0 else ((4 * b + i + 1) // 4) % 2
                                for j in range(T):
                                    g = T * p + j
                                    att.turn(pe, j, g)
                                    if j < 5:
                                        att.scores(pe, s, xx, j + 3, g + 3)
                                    else:
                                        att.scores(pe, 1 - s, xx_next, j - 5, g + 3)
                                    if j < 4:
                                        att.mix_values(pe, 1 - s, 1, j, 2 * p, T * p - 1)
                                    else:
                                        if j == 4:
                                            pe.wait_ge(values_ok, p + 1)
                                        att.mix_values(pe, s, 0, j - 4, 2 * p + 1, T * p + 3)
                                    if j in SPREAD:
                                        spread(pe, p, at, j // 4)
                                    elif j in CAT:
                                        head_out(pe, p, at, j // 4)
                                    elif j in U:
                                        make_u(pe, at + j, j - 2, xx_next, p + 2)
                                    elif j == 7:
                                        project(pe, p, at, w_now[:, HID + 1:])
                    p, at = PASSES, xx_use(B)
                    for quarter in range(4):
                        att.mix_values(pe, 1, 1, quarter, 2 * p, T * p - 1)
                    for half in range(2):
                        spread(pe, p, at + 2 * half - SPREAD[half], half)
                        head_out(pe, p, at + 1 + 2 * half - CAT[half], half)
                    project(pe, p, at + 4 - PROJ, w_now[:, HID + 1:])

                def u_part(a, use, slot, k):
                    a.wait_ge(misc_ok, use + 1)
                    nc.scalar.activation(att.u[:, slot, halves(k)], misc[:], ACT.Copy, scale=-1.0).then_inc(u_high, 1)

                def keep_sum(a, n):
                    a.wait_ge(att.av_ok, n + 2)
                    nc.scalar.activation(o_raw[:], att.o_ps[:], ACT.Copy).then_inc(att.av_used, 1)

                def add_bias(a, p, use, half):
                    if half:
                        a.wait_ge(cat_ok, 2 * p + 1)
                    a.wait_ge(misc_ok, use + 1)
                    nc.scalar.activation(biased[:], misc[:], ACT.Identity, bias=w_now[:, HID:HID + 1])\
                        .then_inc(misc_used, 1)

                def keep_part(a, p, use):
                    a.wait_ge(proj_ok, p + 1)
                    a.wait_ge(misc_ok, use + 1)
                    nc.scalar.activation(part[:], misc[:], ACT.Copy).then_inc(misc_used, 1)

                @block.scalar
                def _(a):
                    for k in range(2):
                        a.wait_ge(misc_ok, k + 1)
                        nc.scalar.activation(att.xx_h[:, 0, halves(k)], misc[:], ACT.Copy).then_inc(xx_high, 1)
                    for k in range(2):
                        u_part(a, 2 + k, 0, k)
                    a.wait_ge(att.start_ok, 5)
                    att.exponents(a, 0, 0, 0)
                    keep_sum(a, -1)
                    with a.Fori(0, B) as b:
                        for k in range(2):
                            wait_apart(a, misc_ok, xx_use(b) + k + 1)
                            nc.scalar.activation(att.xx_h[:, (b + 1) % 2, halves(k)], misc[:], ACT.Copy)\
                                .then_inc(xx_high, 1)
                        with a.Fori(0, H // 2) as i:
                            for s in range(2):
                                p = H * b + 2 * i + s
                                at = base(b, i, s)
                                for j in range(T):
                                    g = T * p + j
                                    if j in (3, 4):
                                        u_part(a, at + U[j - 3], 1 - s, j - 3)
                                    if j == 4:
                                        a.wait_ge(misc_used, at + SPREAD[0] + 2)
                                        keep_sum(a, 2 * p)
                                    if j in (2, 6):
                                        add_bias(a, p, at + CAT[j // 4], j // 4)
                                    if j == 1:
                                        nc.scalar.activation(att.values[:, s], act[:, :, b, :], ACT.Copy)\
                                            .then_inc(values_ok, 1)
                                    att.exponents(a, s if j < T - 1 else 1 - s, (j + 1) % T, g + 1)
                                    att.keep_turned(a, j, g, 2 * p + j // 4)
                                a.wait_ge(misc_used, at + SPREAD[1] + 2)
                                keep_sum(a, 2 * p + 1)
                                keep_part(a, p, at + PROJ)
                    p, at = PASSES, xx_use(B)
                    for half in range(2):
                        if half:
                            a.wait_ge(misc_used, at + 2)
                            keep_sum(a, 2 * p)
                        add_bias(a, p, at + 1 + 2 * half, half)
                    keep_part(a, p, at + 4)

                def make_diag(pool, slot, half, steps):
                    rinv = att.rinv[:, slot, 4 * half:4 * half + 4]
                    high, low = rinv_split[:, 0], rinv_split[:, 1]
                    nc.gpsimd.tensor_copy(high, rinv).then_inc(diag_steps, 1)
                    wait_apart(pool, diag_steps, steps + 1)
                    nc.gpsimd.tensor_tensor(low, rinv, high.bitcast(F32), ALU.subtract).then_inc(diag_steps, 1)
                    wait_apart(pool, diag_steps, steps + 2)
                    for k in range(2):
                        ins = nc.gpsimd.tensor_tensor(
                            diag[:, k], ident[:].unsqueeze(1).to_broadcast([P, 4, P]),
                            rinv_split[:, k].bitcast(F32).unsqueeze(2).to_broadcast([P, 4, P]), ALU.mult)
                    ins.then_inc(diag_ok, 1)

                def stage_x(b):
                    nc.gpsimd.tensor_copy(batch_x[:, :, 0], act[:, :, b, :])
                    nc.gpsimd.tensor_copy(batch_x[:, :, 1], act[:, :, b, :]).then_inc(batch_ok, 1)

                @block.gpsimd
                def _(pool):
                    stage_x(0)
                    nc.gpsimd.tensor_copy(m_now[:], m_split[:, 0, :]).then_inc(m_ok, 1)
                    att.begin_gpsimd(pool)
                    pool.wait_ge(misc_ok, 2)
                    stage_x(1)
                    pool.wait_ge(misc_ok, 4)
                    nc.gpsimd.tensor_copy(m_now[:], m_split[:, 1, :]).then_inc(m_ok, 1)
                    for j in range(2):
                        att.find_zeros_pool(pool, j, j)
                    nc.gpsimd.memset(part[:], 0.0)
                    nc.gpsimd.memset(proj[:], 0.0).then_inc(zeroed, 1)
                    nc.gpsimd.tensor_copy(ones_r[:], ones[:])
                    pool.wait_ge(att.start_ok, 5)
                    make_diag(pool, 0, 0, 0)
                    pool.wait_ge(zeroed, 1)
                    with pool.Fori(0, B) as b:
                        wait_apart(pool, misc_ok, xx_use(b) + 2)
                        stage_x((b + 2) % B)
                        with pool.Fori(0, H // 2) as i:
                            for s in range(2):
                                p = H * b + 2 * i + s
                                at = base(b, i, s)
                                for j in range(2, T + 2):
                                    att.find_zeros_pool(pool, j % T, T * p + j)
                                    if j == 2:
                                        wait_apart(pool, misc_used, at + 1)
                                        nc.gpsimd.tensor_copy(w_now[:], w_heads[:, (2 * i + s + H - 1) % H, :])\
                                            .then_inc(w_ok, 1)
                                    if j == 3:
                                        slot = (H * b + 2 * i + s + H - 2) // H
                                        nc.gpsimd.tensor_tensor(proj[:, slot, :], proj[:, slot, :], part[:], ALU.add)\
                                            .then_inc(proj_ok, 1)
                                    if j == 4:
                                        wait_apart(pool, misc_ok, at + SPREAD[0] + 1)
                                        wait_apart(pool, att.rinv_ok, 2 * p + 1)
                                        make_diag(pool, 1 - s, 1, 4 * p + 2)
                                    if j == 7:
                                        wait_apart(pool, misc_ok, at + U[1] + 1)
                                        nc.gpsimd.tensor_copy(m_now[:], m_split[:, (2 * i + s + 2) % H, :])\
                                            .then_inc(m_ok, 1)
                                    if j == 8:
                                        wait_apart(pool, misc_ok, at + SPREAD[1] + 1)
                                        wait_apart(pool, att.rinv_ok, 2 * p + 2)
                                        make_diag(pool, s, 0, 4 * p + 4)
                    p, at = PASSES, xx_use(B)
                    pool.wait_ge(misc_used, at + 1)
                    nc.gpsimd.tensor_copy(w_now[:], w_heads[:, H - 1, :]).then_inc(w_ok, 1)
                    nc.gpsimd.tensor_tensor(proj[:, B, :], proj[:, B, :], part[:], ALU.add).then_inc(proj_ok, 1)
                    pool.wait_ge(misc_ok, at + 1)
                    pool.wait_ge(att.rinv_ok, 2 * p + 1)
                    make_diag(pool, 1, 1, 4 * p + 2)
                    pool.wait_ge(misc_used, at + 6)
                    pool.wait_ge(proj_ok, p + 1)
                    nc.gpsimd.tensor_tensor(proj[:, B, :], proj[:, B, :], part[:], ALU.add).then_inc(proj_ok, 1)

                def u_low(v, count, slot, k):
                    v.wait_ge(u_high, count)
                    nc.vector.scalar_tensor_tensor(out=att.u[C:P, slot, halves(k)], in0=misc[C:P, :], scalar=-1.0,
                                                   in1=att.u[C:P, slot, halves(k)].bitcast(F32), op0=ALU.mult,
                                                   op1=ALU.subtract).then_inc(misc_used, 1)

                def normalise(v, p, use, half):
                    v.wait_ge(att.av_used, 2 * p + half + 1)
                    v.wait_ge(misc_ok, use + 1)
                    nc.vector.tensor_tensor(o_norm[:], o_raw[:], misc[:], ALU.mult).then_inc(misc_used, 1)

                def leaky(v, use, half):
                    v.wait_ge(misc_used, use + 2)
                    nc.vector.scalar_tensor_tensor(out=cat[:, halves(half)], in0=biased[:], scalar=SLOPE,
                                                   in1=biased[:], op0=ALU.mult, op1=ALU.max).then_inc(cat_ok, 1)

                @block.vector
                def _(v):
                    att.begin(v)
                    for k in range(2):
                        v.wait_ge(xx_high, k + 1)
                        nc.vector.tensor_tensor(att.xx_l[:, 0, halves(k)], misc[:],
                                                att.xx_h[:, 0, halves(k)].bitcast(F32), ALU.subtract)\
                            .then_inc(misc_used, 1)
                    for k in range(2):
                        u_low(v, k + 1, 0, k)
                    for j in range(2):
                        att.multiply(v, j, j)
                        att.find_zeros(v, j, j)
                    att.mask(v, 0, 0, 0)
                    with v.Fori(0, B) as b:
                        for k in range(2):
                            v.wait_ge(xx_high, 2 * b + k + 3)
                            nc.vector.tensor_tensor(att.xx_l[:, (b + 1) % 2, halves(k)], misc[:],
                                                    att.xx_h[:, (b + 1) % 2, halves(k)].bitcast(F32), ALU.subtract)\
                                .then_inc(misc_used, 1)
                        with v.Fori(0, H // 2) as i:
                            for s in range(2):
                                p = H * b + 2 * i + s
                                at = base(b, i, s)
                                for j in range(2, T + 2):
                                    g = T * p + j
                                    if j == 4:
                                        normalise(v, p, at + SPREAD[0], 0)
                                    if j in (6, 7):
                                        u_low(v, 2 * p + j - 3, 1 - s, j - 6)
                                    if j == 8:
                                        normalise(v, p, at + SPREAD[1], 1)
                                    if j in (5, 9):
                                        leaky(v, at + CAT[j // 8], j // 8)
                                    att.multiply(v, j % T, g)
                                    att.mask(v, s if j <= T else 1 - s, (j - 1) % T, g - 1)
                                    att.find_zeros(v, j % T, g)
                                    if j == 2:
                                        att.invert(v, 1 - s, 1, T * p)
                                    if j == 5:
                                        att.invert(v, s, 0, T * p + 4)
                    p, at = PASSES, xx_use(B)
                    att.invert(v, 1, 1, T * p)
                    for half in range(2):
                        normalise(v, p, at + 2 * half, half)
                        leaky(v, at + 1 + 2 * half, half)

        def output_attention(proj):
            with ExitStack() as ctx:
                att = Attention(ctx, "o", 2)
                g_now = sb("g_now", [P, HN], ctx=ctx)
                o_sb = sb("o_sb", [P, HN], ctx=ctx)
                y = sb("y", [P, 2, 4, C], ctx=ctx)
                g_ok, xx_high, u_ok, y_steps, added = sems(ctx, "g_ok", "xx_high_o", "u_ok", "y_steps", "added")
                block = ctx.enter_context(nc.Block())
                misc, misc_ok, misc_used = att.misc, att.misc_ok, att.misc_used

                USES = 5
                OUT, X, VALUES = (0, 3), (1, 2), 4

                def base(p):
                    return 3 + USES * p

                def halves(k):
                    return slice(k * HN, (k + 1) * HN)

                @block.gpsimd
                def _(pool):
                    nc.gpsimd.tensor_copy(g_now[:], proj[:, 1, :]).then_inc(g_ok, 1)
                    att.begin_gpsimd(pool)
                    pool.wait_ge(misc_ok, 3)
                    nc.gpsimd.tensor_copy(g_now[:], proj[:, 2, :]).then_inc(g_ok, 1)
                    for j in range(2):
                        att.find_zeros_pool(pool, j, j)
                    with pool.Fori(0, B // 2) as i:
                        for s in range(2):
                            p = 2 * i + s
                            for j in range(2, T + 2):
                                att.find_zeros_pool(pool, j % T, T * p + j)
                            wait_apart(pool, misc_ok, base(p) + VALUES + 1)
                            nc.gpsimd.tensor_copy(g_now[:], proj[:, (p + 2) % B + 1, :]).then_inc(g_ok, 1)

                def spread_x(pe, use, k, count):
                    pe.wait_ge(g_ok, count)
                    pe.wait_ge(misc_used, use + 1)
                    nc.tensor.matmul(misc[:], fold[k * C:(k + 1) * C, :], g_now[k * C:(k + 1) * C, :],
                                     start=True, stop=True).then_inc(misc_ok, 1)

                def turn_values(pe, use):
                    pe.wait_ge(misc_used, use + 1)
                    for m in range(4):
                        ins = nc.tensor.transpose(misc[:, m * P:(m + 1) * P], g_now[:, m * P:(m + 1) * P], ident[:])
                    ins.then_inc(misc_ok, 1)

                def turn_out(pe, p, use, half):
                    pe.wait_ge(misc_used, use + 1)
                    pe.wait_ge(att.av_used, 2 * p + half + 1)
                    for m in range(4):
                        ins = nc.tensor.matmul(misc[:, m * C:(m + 1) * C], o_sb[:, m * P:(m + 1) * P], fold[:, 0:C],
                                               start=True, stop=True, skip_group_check=True)
                    ins.then_inc(misc_ok, 1)

                @block.tensor
                def _(pe):
                    for k in range(2):
                        spread_x(pe, k, k, 1)
                    turn_values(pe, 2)
                    pe.wait_ge(u_ok, 2)
                    for j in range(3):
                        att.scores(pe, 0, 0, j, j)
                    pe.wait_ge(att.start_ok, 5)
                    with pe.Fori(0, B // 2) as i:
                        for s in range(2):
                            p = 2 * i + s
                            at = base(p)
                            for j in range(T):
                                g = T * p + j
                                att.turn(pe, j, g)
                                if j < 5:
                                    att.scores(pe, s, s, j + 3, g + 3)
                                else:
                                    if j == 5:
                                        pe.wait_ge(u_ok, 2 * p + 4)
                                    att.scores(pe, 1 - s, 1 - s, j - 5, g + 3)
                                if j < 4:
                                    att.mix_values(pe, 1 - s, 1, j, 2 * p, T * p - 1)
                                else:
                                    att.mix_values(pe, s, 0, j - 4, 2 * p + 1, T * p + 3)
                                if j == 0:
                                    turn_out(pe, p, at + OUT[0], 0)
                                elif j in (1, 2):
                                    spread_x(pe, at + X[j - 1], j - 1, p + 2)
                                elif j == 5:
                                    turn_out(pe, p, at + OUT[1], 1)
                                elif j == 6:
                                    turn_values(pe, at + VALUES)
                    p, at = B, base(B)
                    turn_out(pe, p, at, 0)
                    for quarter in range(4):
                        att.mix_values(pe, 1, 1, quarter, 2 * p, T * p - 1)
                    turn_out(pe, p, at + 1, 1)

                def x_high(a, use, slot, k):
                    a.wait_ge(misc_ok, use + 1)
                    nc.scalar.activation(att.u[0:C, slot, halves(k)], misc[0:C, :], ACT.Copy, scale=-1.0)
                    nc.scalar.activation(att.xx_h[:, slot, halves(k)], misc[:], ACT.Copy).then_inc(xx_high, 1)

                def u_low(a, use, slot, k):
                    a.wait_ge(misc_used, use + 2)
                    nc.scalar.activation(att.u[C:P, slot, halves(k)], att.xx_l[C:P, slot, halves(k)].bitcast(F32),
                                         ACT.Copy, scale=-1.0).then_inc(u_ok, 1)

                def keep_values(a, use, slot):
                    a.wait_ge(misc_ok, use + 1)
                    nc.scalar.activation(att.values[:, slot].rearrange("p (a m) c -> p m a c", a=2),
                                         misc[:].rearrange("p (m a c) -> p m a c", m=4, a=2),
                                         ACT.Copy).then_inc(misc_used, 1)

                def keep_sum(a, n):
                    a.wait_ge(att.av_ok, n + 2)
                    nc.scalar.activation(o_sb[:], att.o_ps[:], ACT.Copy).then_inc(att.av_used, 1)

                @block.scalar
                def _(a):
                    for k in range(2):
                        x_high(a, k, 0, k)
                        u_low(a, k, 0, k)
                    keep_values(a, 2, 0)
                    a.wait_ge(att.start_ok, 5)
                    att.exponents(a, 0, 0, 0)
                    keep_sum(a, -1)
                    with a.Fori(0, B // 2) as i:
                        for s in range(2):
                            p = 2 * i + s
                            at = base(p)
                            for j in range(T):
                                g = T * p + j
                                if j in (2, 3):
                                    x_high(a, at + X[j - 2], 1 - s, j - 2)
                                if j in (3, 4):
                                    u_low(a, at + X[j - 3], 1 - s, j - 3)
                                if j == 4:
                                    a.wait_ge(misc_ok, at + OUT[0] + 1)
                                    keep_sum(a, 2 * p)
                                att.exponents(a, s if j < T - 1 else 1 - s, (j + 1) % T, g + 1)
                                att.keep_turned(a, j, g, 2 * p + j // 4)
                            keep_values(a, at + VALUES, 1 - s)
                            keep_sum(a, 2 * p + 1)
                    a.wait_ge(misc_ok, base(B) + 1)
                    keep_sum(a, 2 * B)

                @block.vector
                def _(v):
                    att.begin(v)
                    steps = Count(y_steps)

                    def x_low(count, slot, k):
                        v.wait_ge(xx_high, count)
                        nc.vector.tensor_tensor(att.xx_l[:, slot, halves(k)], misc[:],
                                                att.xx_h[:, slot, halves(k)].bitcast(F32), ALU.subtract)\
                            .then_inc(misc_used, 1)

                    def finish(p, use, slot, half):
                        rinv = att.rinv[:, slot, 4 * half:4 * half + 4]
                        v.wait_ge(misc_ok, use + 1)
                        v.wait_ge(att.rinv_ok, 2 * p + 1)
                        nc.vector.tensor_tensor(y[:, 0], misc[:, 0:4 * C].rearrange("p (m c) -> p m c", m=4),
                                                rinv.unsqueeze(2).to_broadcast([P, 4, C]), ALU.mult)\
                            .then_inc(misc_used, 1)
                        v.wait_ge(misc_used, use + 2)
                        steps.add(nc.vector.tensor_tensor(
                            y[:, 1], y[:, 0], b_proj[:].unsqueeze(1).to_broadcast([P, 4, C]), ALU.add))
                        v.wait_ge(y_steps, steps.value)
                        steps.add(nc.vector.scalar_tensor_tensor(
                            out=proj[:, p, 4 * C * half:4 * C * (half + 1)].rearrange("p (m c) -> p m c", m=4),
                            in0=y[:, 1], scalar=SLOPE, in1=y[:, 1], op0=ALU.mult, op1=ALU.max))

                    for k in range(2):
                        x_low(k + 1, 0, k)
                    for j in range(2):
                        att.multiply(v, j, j)
                        att.find_zeros(v, j, j)
                    att.mask(v, 0, 0, 0)
                    with steps.over(v, B // 2, 8) as i:
                        for s in range(2):
                            p = 2 * i + s
                            at = base(p)
                            for j in range(2, T + 2):
                                g = T * p + j
                                if j in (5, 6):
                                    x_low(2 * p + j - 2, 1 - s, j - 5)
                                if j == 4:
                                    finish(p, at + OUT[0], 1 - s, 0)
                                if j == 9:
                                    finish(p, at + OUT[1], 1 - s, 1)
                                att.multiply(v, j % T, g)
                                att.mask(v, s if j <= T else 1 - s, (j - 1) % T, g - 1)
                                att.find_zeros(v, j % T, g)
                                if j == 2:
                                    att.invert(v, 1 - s, 1, T * p)
                                if j == 5:
                                    att.invert(v, s, 0, T * p + 4)
                    p, at = B, base(B)
                    att.invert(v, 1, 1, T * p)
                    for half in range(2):
                        finish(p, at + half, 1, half)
                    v.wait_ge(y_steps, steps.value)
                    nc.vector.tensor_tensor(res[:], res[:],
                                            proj[:, 1:1 + B].rearrange("p b (t c) -> p t b c", t=T), ALU.add)\
                        .then_inc(added, 1)
                    v.wait_ge(added, 1)


        def split_tiles(ctx, *names):
            return [sb(n, [P, T, B, C], F32R, ctx=ctx) for n in names]

        with ExitStack() as ctx:
            high, low = split_tiles(ctx, "high", "low")
            y1 = sb("y1", [P, T, B, C], ctx=ctx)
            with ExitStack() as layer0:
                y2 = sb("y2", [P, T, B, C], ctx=layer0)
                prepare(high, low)
                with ExitStack() as split:
                    y_high, y_low = split_tiles(split, "y1_high", "y1_low")
                    graph_product("0", high, low, KeepSplit(y1, y_high, y_low), degrees=True)
                    graph_product("1", y_high, y_low, Chebyshev(y2, act))
                node_weights(y1, y2)
            layernorm("1", 4, 4, high, low, scaled=y1)
            graph_product("2", high, low, Mix(bd1[:], "residual", scaled=y1))
            layernorm("2", 8, 8, None, None)
        with ExitStack() as ctx:
            proj = sb("proj", [P, 1 + B, HN], ctx=ctx)
            heads(proj)
            output_attention(proj)
        with ExitStack() as ctx:
            high, low, y_high, y_low = split_tiles(ctx, "high3", "low3", "y_high3", "y_low3")
            layernorm("3", 12, 8, high, low)
            graph_product("3", high, low, Mix(bd3[:, 0], "split", y_high=y_high, y_low=y_low))
            graph_product("4", y_high, y_low, Mix(bd3[:, 1], "store"))


_INS = ["x", "adj", "L0_gnn_embedding", "L0_gnn_weight", "L0_gnn_bias", "L1_gnn_W", "L2_gnn_Wh", "L2_gnn_bh",
        "L2_gnn_W_out", "L2_gnn_b_out", "L3_gnn_net_params"]


def kernel(**inputs):
    import numpy as _np
    import concourse.bacc as _bacc
    from concourse.bass_utils import run_bass_kernel_spmd as _run

    nc = _bacc.Bacc("TRN2", target_bir_lowering=False, num_devices=1)
    arrays, args = {}, []
    for name in _INS:
        a = _np.ascontiguousarray(inputs[name])
        arrays[f"in_{name}"] = a
        args.append(nc.dram_tensor(f"in_{name}", a.shape, mybir.dt.from_np(a.dtype), kind="ExternalInput").ap())
    out = nc.dram_tensor("out", inputs["x"].shape, F32, kind="ExternalOutput").ap()
    build_kernel(nc, *args, out)
    return _run(nc, [arrays], core_ids=[0]).results[0]["out"]
```
